# Optimizing a Trainium2 kernel written in Bass

```python
import numpy as np
import jax
import jax.numpy as jnp

def _softmax(x, axis=-1):
    return jax.nn.softmax(x, axis=axis)

def _gelu(x):
    return jax.nn.gelu(x, approximate=True)

def _silu(x):
    return jax.nn.silu(x)

def _sigmoid(x):
    return jax.nn.sigmoid(x)

def _layernorm(x, axis=-1, eps=1e-05):
    m = jnp.mean(x, axis=axis, keepdims=True)
    v = jnp.var(x, axis=axis, keepdims=True)
    return (x - m) / jnp.sqrt(v + eps)

def _scatter_add(tgt, idx, src, axis=0):
    return tgt.at[idx].add(src)

def _segment_sum(src, seg, n):
    return jax.ops.segment_sum(src, seg, n)
kernel_name = 'mk_seq_postln_d1_jaxref_r4_cb6094'

def setup_inputs(seed: int=0):
    np.random.seed(seed)
    _w = jnp.asarray

    def _L0_attn_setup():
        import jax, jax.numpy as jnp
        import numpy as np
        B, T, D = (4, 1024, 256)

        def _rmsnorm(y, w):
            return y * jax.lax.rsqrt(jnp.mean(y * y, axis=-1, keepdims=True) + 1e-06) * w
        key = jax.random.key(seed)
        ks = jax.random.split(key, 6)
        std = np.sqrt(2.0 / D).astype(np.float32)
        return {'x': jax.random.normal(ks[0], (B, T, D), dtype=jnp.float32), 'Wr': jax.random.normal(ks[1], (D, D), dtype=jnp.float32) * std, 'Wk': jax.random.normal(ks[2], (D, D), dtype=jnp.float32) * std, 'Wv': jax.random.normal(ks[3], (D, D), dtype=jnp.float32) * std, 'Wo': jax.random.normal(ks[4], (D, D), dtype=jnp.float32) * std, 'decay': jnp.ones((D,), dtype=jnp.float32) * 0.99, 'ln_w': jnp.ones((D,), dtype=jnp.float32)}
    _L0_attn_in = _L0_attn_setup()

    def _L0_ffn_setup():
        import jax, jax.numpy as jnp
        import numpy as np

        def _binarize(w):
            alpha = jax.lax.stop_gradient(jnp.mean(jnp.abs(w), axis=1, keepdims=True))
            bw = alpha * jnp.sign(w)
            return w + jax.lax.stop_gradient(bw - w)
        key = jax.random.key(seed)
        k1, k2, k3, k4, k5 = jax.random.split(key, 5)
        D, H = (256, 1024)
        x = jax.random.normal(k1, (64, 196, D), dtype=jnp.float32)
        w1 = jax.random.normal(k2, (H, D), dtype=jnp.float32) * 0.02
        b1 = jax.random.normal(k3, (H,), dtype=jnp.float32) * 0.02
        w2 = jax.random.normal(k4, (D, H), dtype=jnp.float32) * 0.02
        b2 = jax.random.normal(k5, (D,), dtype=jnp.float32) * 0.02
        return {'x': x, 'w1': w1, 'b1': b1, 'w2': w2, 'b2': b2}
    _L0_ffn_in = _L0_ffn_setup()
    _d = {'L0_attn_x': _L0_attn_in['x'], 'L0_attn_Wr': _L0_attn_in['Wr'], 'L0_attn_Wk': _L0_attn_in['Wk'], 'L0_attn_Wv': _L0_attn_in['Wv'], 'L0_attn_Wo': _L0_attn_in['Wo'], 'L0_attn_decay': _L0_attn_in['decay'], 'L0_attn_ln_w': _L0_attn_in['ln_w'], 'L0_ffn_w1': _L0_ffn_in['w1'], 'L0_ffn_b1': _L0_ffn_in['b1'], 'L0_ffn_w2': _L0_ffn_in['w2'], 'L0_ffn_b2': _L0_ffn_in['b2']}
    _x0 = _d['L0_attn_x']
    _d['L0_attn_x'] = jax.random.normal(jax.random.fold_in(jax.random.key(seed), 1), (8, 2048, 256), dtype=_x0.dtype)
    del _x0
    return _d

def reference(L0_attn_x, L0_attn_Wr, L0_attn_Wk, L0_attn_Wv, L0_attn_Wo, L0_attn_decay, L0_attn_ln_w, L0_ffn_w1, L0_ffn_b1, L0_ffn_w2, L0_ffn_b2):

    def _L0_attn_ref(x, Wr, Wk, Wv, Wo, decay, ln_w):
        import jax, jax.numpy as jnp
        import numpy as np
        B, T, D = (4, 1024, 256)

        def _rmsnorm(y, w):
            return y * jax.lax.rsqrt(jnp.mean(y * y, axis=-1, keepdims=True) + 1e-06) * w
        Bsz, Tlen, Dm = x.shape
        r = jax.nn.sigmoid(jnp.einsum('btd,ed->bte', x, Wr))
        k = jnp.einsum('btd,ed->bte', x, Wk)
        v = jnp.einsum('btd,ed->bte', x, Wv)
        dec = jax.nn.sigmoid(decay)
        log_decay = jnp.log(jnp.clip(dec, 1e-07))
        t = jnp.arange(Tlen, dtype=x.dtype)[:, None]
        scale = jnp.exp(t * log_decay[None, :])
        kv = k * v
        cum = jnp.cumsum(kv / jnp.clip(scale, 1e-10)[None], axis=1)
        state = cum * scale[None]
        y = _rmsnorm(r * state, ln_w)
        return jnp.einsum('btd,ed->bte', y, Wo)

    def _L0_ffn_ref(x, w1, b1, w2, b2):
        import jax, jax.numpy as jnp
        import numpy as np

        def _binarize(w):
            alpha = jax.lax.stop_gradient(jnp.mean(jnp.abs(w), axis=1, keepdims=True))
            bw = alpha * jnp.sign(w)
            return w + jax.lax.stop_gradient(bw - w)
        bw1 = _binarize(w1)
        h = jnp.einsum('bsd,hd->bsh', x, bw1) + b1
        h = jax.nn.gelu(h, approximate=False)
        bw2 = _binarize(w2)
        out = jnp.einsum('bsh,dh->bsd', h, bw2) + b2
        return out
    x = L0_attn_x
    x = _layernorm(x + _L0_attn_ref(x, L0_attn_Wr, L0_attn_Wk, L0_attn_Wv, L0_attn_Wo, L0_attn_decay, L0_attn_ln_w), axis=-1)
    x = _layernorm(x + _L0_ffn_ref(x, L0_ffn_w1, L0_ffn_b1, L0_ffn_w2, L0_ffn_b2), axis=-1)
    return x

_drawn_inputs = setup_inputs


def setup_inputs(seed=0):
    import zlib

    import numpy as np

    out = dict(_drawn_inputs(seed))
    spreads = {'L0_attn_decay': (0.9900000095367432, 0.2), 'L0_attn_ln_w': (1.0, 0.2)}
    factors = {'L0_ffn_b1': 8.0, 'L0_ffn_b2': 2.923}
    for name, (base, spread) in spreads.items():
        noise = np.random.default_rng([zlib.crc32(name.encode()), seed]).standard_normal(out[name].shape)
        drawn = base * np.exp(spread * noise) if base else spread * noise
        out[name] = jnp.asarray(drawn.astype(out[name].dtype))
    for name, factor in factors.items():
        out[name] = (out[name] * factor).astype(out[name].dtype)
    return out
```

```python
import concourse.bass as bass
from concourse import mybir
from contextlib import ExitStack

P = 128


def postln_layer_kernel(nc, x, Wr, Wk, Wv, Wo, decay, ln_w, w1, b1, w2, b2, out):
    fp32, fp16, i32 = mybir.dt.float32, mybir.dt.float16, mybir.dt.int32
    ALU, ACT, AX = mybir.AluOpType, mybir.ActivationFunctionType, mybir.AxisListType
    RMAX = bass.bass_isa.ReduceOp.max

    B, T, D = x.shape
    H = w1.shape[0]
    CH = 512
    CPB = T // CH
    NCH = B * CPB
    TT = CH // P
    DC = D // P
    HC = H // P
    NHF = 4
    TOP = 16384.0
    X1S = 2048.0
    HTOP = 32768.0
    TINY = 1e-30
    EPS_RMS, EPS_LN = 1e-6, 1e-5
    CLIP_SCALE, LOG_CLIP = 1e-10, 23.025850929940457
    CLIP_DEC = 1e-7

    x_v = x.rearrange("b (c tt p) d -> (b c) p tt d", c=CPB, p=P)
    out_v = out.rearrange("b (c tt p) d -> (b c) p tt d", c=CPB, p=P)

    ctx = ExitStack()
    with ctx:
        def sb(name, shape, dt=fp32):
            return ctx.enter_context(nc.sbuf_tensor(name, shape, dt))

        def sem(name):
            return ctx.enter_context(nc.semaphore(name))

        ident = sb("ident", [P, P])
        ident16 = sb("ident16", [P, P], fp16)
        ones_col = sb("ones_col", [P, 1])
        ones_sq = sb("ones_sq", [P, P])
        proj_hi = sb("proj_hi", [P, 3, DC, D], fp16)
        proj_lo = sb("proj_lo", [P, 3, DC, D], fp16)
        woT = sb("woT", [P, DC, D])
        w1T = sb("w1T", [P, DC, H], fp16)
        w2T = sb("w2T", [P, HC, D], fp16)
        f1_scale = sb("f1_scale", [P, HC])
        b1c = sb("b1c", [P, HC])
        b2r = sb("b2r", [P, D])
        alpha2r = sb("alpha2r", [P, D])
        hid_scale = sb("hid_scale", [P, 1])
        decay_f = sb("decay_f", [P, DC, CH])
        clip_g = sb("clip_g", [P, DC, T])
        w_inv = sb("w_inv", [P, 3])

        proj_in = sb("proj_in", [P, 3, DC, D])
        wo_in = sb("wo_in", [P, DC, D])
        w1_in = sb("w1_in", [P, HC, D])
        w2_in = sb("w2_in", [P, DC, H])
        w1_sgn = sb("w1_sgn", [P, HC, D], fp16)
        w2_sgn = sb("w2_sgn", [P, DC, H], fp16)
        steps = sb("steps", [P, T])
        lnw_c = sb("lnw_c", [P, DC])
        dec_c = sb("dec_c", [P, 3, DC])
        log_clip = sb("log_clip", [P, 1])
        w_max = sb("w_max", [P, 4])
        w_amax = sb("w_amax", [P, 4])
        w_scl = sb("w_scl", [P, 4])
        alpha1 = sb("alpha1", [P, HC])
        alpha2 = sb("alpha2", [P, DC])
        hid_bound = sb("hid_bound", [P, 2, HC])
        alpha2_sq = sb("alpha2_sq", [P, DC, P])

        x_in = [sb(f"x_in{n}", [P, TT, D]) for n in range(CPB)]
        x_max = sb("x_max", [P, CPB, 2])
        x_scl = sb("x_scl", [P, CPB, 5])
        x_hi = sb("x_hi", [P, DC, CH], fp16)
        x_lo = sb("x_lo", [P, DC, CH], fp16)
        r_tanh = sb("r_tanh", [P, DC, CH])
        k_sb = sb("k_sb", [P, DC, CH])
        kv = sb("kv", [P, DC, CH])
        kvg = sb("kvg", [P, DC, CH])
        state = [sb(f"state{n}", [P, DC, CH]) for n in range(2)]
        y = sb("y", [P, DC, CH])
        y_sq = sb("y_sq", [P, DC, CH])
        y_sqs = sb("y_sqs", [P, CH])
        ms = sb("ms", [P, TT])
        rms = sb("rms", [P, TT])
        u = sb("u", [P, TT, D])
        u_st = sb("u_st", [P, TT, 6])
        u_mv = sb("u_mv", [P, TT, 2])
        u_ve = sb("u_ve", [P, TT])
        u_rstd = sb("u_rstd", [P, TT])
        x1 = sb("x1", [P, TT, D])
        x1b = [sb(f"x1b{n}", [P, TT, D]) for n in range(2)]
        x1_hi = sb("x1_hi", [P, DC, CH], fp16)
        x1_lo = sb("x1_lo", [P, DC, CH], fp16)
        hid = sb("hid", [P, NHF, CH])
        hid_hi = sb("hid_hi", [P, HC, CH], fp16)
        hid_lo = sb("hid_lo", [P, HC, CH], fp16)
        z = [sb(f"z{n}", [P, TT, D]) for n in range(2)]
        z_st = sb("z_st", [P, TT, 6])
        z_mv = sb("z_mv", [P, TT, 2])
        z_ve = sb("z_ve", [P, TT])
        z_rstd = sb("z_rstd", [P, TT])
        z_out = [sb(f"z_out{n}", [P, TT, D]) for n in range(2)]
        neg_one = sb("neg_one", [P, 1])
        neg_half = sb("neg_half", [P, TT])

        ps_o = ctx.enter_context(nc.psum_tensor("ps_o", [P, 2, CH], fp32))
        ps_f = ctx.enter_context(nc.psum_tensor("ps_f", [P, 2, CH], fp32))
        ps_r = ctx.enter_context(nc.psum_tensor("ps_r", [P, 3, CH], fp32))
        ps_s = ctx.enter_context(nc.psum_tensor("ps_s", [P, CH], fp32))
        o_tok = ps_o[:, :, :].rearrange("p a (b d) -> p (a b) d", d=D)

        s_proj_in, s_wo_in, s_w1_in, s_w2_in = (sem(n) for n in ("proj_in_s", "wo_in_s", "w1_in_s", "w2_in_s"))
        s_small_in = sem("small_in_s")
        s_zeroed, s_ident, s_const = sem("zeroed_s"), sem("ident_s"), sem("const_s")
        s_wmax, s_wamax = sem("wmax_s"), sem("wamax_s")
        s_setup_pe, s_setup_ev, s_setup_v, s_setup_a = (sem(n) for n in ("setup_pe", "setup_ev", "setup_v", "setup_a"))
        s_sgn, s_wcopy, s_ready = sem("sgn_s"), sem("wcopy_s"), sem("weights_ready_s")
        s_passed = [sem("passed_pool_s"), sem("passed_dve_s")]
        s_x_in = [sem(f"x_in_s{n}") for n in range(CPB)]
        s_xmax, s_xscl = sem("xmax_s"), sem("xscl_s")
        s_xamax = sem("xamax_s")
        s_xtmp = sem("xtmp_s")
        s_tx, s_xh, s_xl = sem("tx_s"), sem("xh_s"), sem("xl_s")
        s_proj, s_rk, s_kv, s_kvg = sem("proj_s"), sem("rk_s"), sem("kv_s"), sem("kvg_s")
        s_scan, s_y, s_ysq, s_ysqs = sem("scan_s"), sem("y_s"), sem("ysq_s"), sem("ysqs_s")
        s_o, s_ms, s_rms, s_u = sem("o_s"), sem("ms_s"), sem("rms_s"), sem("u_s")
        s_ust, s_umv, s_uve, s_urstd = sem("ust_s"), sem("umv_s"), sem("uve_s"), sem("urstd_s")
        s_x1, s_x1b, s_t1, s_x1h, s_x1l = sem("x1_s"), sem("x1b_s"), sem("t1_s"), sem("x1h_s"), sem("x1l_s")
        s_f1, s_gelu, s_hh, s_hl = sem("f1_s"), sem("gelu_s"), sem("hh_s"), sem("hl_s")
        s_f2, s_zmul, s_zadd = sem("f2_s"), sem("zmul_s"), sem("zadd_s")
        s_zst, s_zmv, s_zve, s_zrstd, s_zout = sem("zst_s"), sem("zmv_s"), sem("zve_s"), sem("zrstd_s"), sem("zout_s")
        s_stored = [sem(f"stored_s{n}") for n in range(2)]

        def stand_alone(eng):
            eng.sem_inc(s_passed[eng is nc.vector], 1)

        def steps_of(eng, prologue, step):
            prologue()
            with eng.Fori(0, B - 1) as b:
                for j in range(CPB):
                    step(b * CPB + j, b, j, NCH)
            for j in range(CPB):
                step((B - 1) * CPB + j, B - 1, j, CPB - j)


        block = ctx.enter_context(nc.Block())

        @block.sync
        def _(sp):
            def load(c, b, j):
                sp.dma_start(x_in[j][:, :, :], x_v[c]).then_inc(s_x_in[j], 16)

            for n in range(2):
                sp.sem_inc(s_stored[n], 16)
            load(0, 0, 0)
            for n, w in enumerate((Wr, Wk, Wv)):
                sp.dma_start(proj_in[:, n], w.rearrange("(c p) d -> p c d", p=P)).then_inc(s_proj_in, 16)
            load(1, 0, 1)
            sp.dma_start(wo_in[:, :, :], Wo.rearrange("(c p) d -> p c d", p=P)).then_inc(s_wo_in, 16)
            load(2, 0, 2)
            sp.dma_start(w1_in[:, :, :], w1.rearrange("(c p) d -> p c d", p=P)).then_inc(s_w1_in, 16)
            sp.dma_start(w2_in[:, :, :], w2.rearrange("(c p) h -> p c h", p=P)).then_inc(s_w2_in, 16)
            load(3, 0, 3)

            def step(i, b, j, left):
                if left > 4:
                    sp.wait_ge(s_u, TT * i + TT)
                    load(i + 4, b + 1, j)
                sp.wait_ge(s_zout, TT * i + TT)
                sp.dma_start(out_v[i], z_out[j % 2][:, :, :]).then_inc(s_stored[j % 2], 16)

            steps_of(sp, lambda: None, step)
            for n in range(2):
                sp.wait_ge(s_stored[n], 16 + 16 * NCH // 2)

        @block.tensor
        def _(pe):
            def transposes(dst, src, c):
                for dc in range(DC):
                    for tt in range(TT):
                        last = nc.tensor.transpose(dst[:, dc, tt * P:(tt + 1) * P],
                                                   src[:, tt, dc * P:(dc + 1) * P], ident[:, :])
                return last

            def TX(c, b, j, first=False):
                if not first:
                    pe.wait_ge(s_rk, 4 * c)
                pe.wait_ge(s_x_in[j], 16 * b + 16)
                transposes(ps_r, x_in[j], c).then_inc(s_tx, 1)

            def R(c, first):
                pe.wait_ge(s_xh, c + 1)
                pe.wait_ge(s_xl, c + 1)
                for ec in range(DC):
                    for m in range(3):
                        if m < 2 and ec:
                            pe.wait_ge(s_rk, 4 * c + m + 1)
                        if m == 2 and (ec or not first):
                            pe.wait_ge(s_kv, 2 * c + ec)
                        n = 0
                        for w, xx in ((proj_hi, x_hi), (proj_hi, x_lo), (proj_lo, x_hi)):
                            for dc in range(DC):
                                last = nc.tensor.matmul(ps_r[:, m, :], w[:, m, dc, ec * P:(ec + 1) * P],
                                                        xx[:, dc, :], start=(n == 0), stop=(n == 3 * DC - 1))
                                n += 1
                        last.then_inc(s_proj, 1)

            def O(c, k):
                pe.wait_ge(s_y, 2 * c + 2)
                if k >= 2:
                    pe.wait_ge(s_zmul, 2 * c - 2)
                elif k == 1:
                    pe.wait_ge(s_u, TT)
                for tt in range(TT):
                    for dc in range(DC):
                        nc.tensor.matmul(o_tok[:, tt, :], y[:, dc, tt * P:(tt + 1) * P], woT[:, dc, :],
                                         start=(dc == 0), stop=(dc == DC - 1))
                pe.wait_ge(s_ysqs, c + 1)
                if k:
                    pe.wait_ge(s_ms, c)
                for tt in range(TT):
                    last = nc.tensor.matmul(ps_s[:, tt:tt + 1], y_sqs[:, tt * P:(tt + 1) * P], ones_col[:, :],
                                            start=True, stop=True)
                last.then_inc(s_o, 1)

            def T1(c, first):
                pe.wait_ge(s_x1, TT * c + TT)
                if not first:
                    pe.wait_ge(s_gelu, HC * c)
                transposes(ps_f, x1, c).then_inc(s_t1, 1)

            def F1(c):
                pe.wait_ge(s_x1h, c + 1)
                pe.wait_ge(s_x1l, c + 1)
                for hc in range(HC):
                    if hc >= 2:
                        pe.wait_ge(s_gelu, HC * c + hc - 1)
                    for dc in range(DC):
                        for n, xx in enumerate((x1_hi, x1_lo)):
                            last = nc.tensor.matmul(ps_f[:, hc % 2, :], w1T[:, dc, hc * P:(hc + 1) * P],
                                                    xx[:, dc, :], start=(dc == 0 and n == 0),
                                                    stop=(dc == DC - 1 and n == 1))
                    last.then_inc(s_f1, 1)

            def F2(c, left):
                if left > 1:
                    pe.wait_ge(s_u, TT * c + 2 * TT)
                for tt in range(TT):
                    for hc in range(HC):
                        if tt == 0:
                            pe.wait_ge(s_hl, HC * c + hc + 1)
                        for n, hh in enumerate((hid_hi, hid_lo)):
                            last = nc.tensor.matmul(o_tok[:, tt, :], hh[:, hc, tt * P:(tt + 1) * P],
                                                    w2T[:, hc, :], start=(hc == 0 and n == 0),
                                                    stop=(hc == HC - 1 and n == 1))
                    if tt % 2:
                        last.then_inc(s_f2, 1)

            pe.wait_ge(s_ident, 2)
            for n in range(3):
                pe.wait_ge(s_proj_in, 48)
                for dc in range(DC):
                    for ec in range(DC):
                        last = nc.tensor.transpose(ps_r[:, n, dc * D + ec * P:dc * D + (ec + 1) * P],
                                                   proj_in[:, n, ec, dc * P:(dc + 1) * P], ident[:, :])
                last.then_inc(s_setup_pe, 1)
            def other_weights():
                pe.wait_ge(s_wo_in, 16)
                for dc in range(DC):
                    for ec in range(DC):
                        last = nc.tensor.transpose(ps_s[:, dc * D + ec * P:dc * D + (ec + 1) * P],
                                                   wo_in[:, ec, dc * P:(dc + 1) * P], ident[:, :])
                last.then_inc(s_setup_pe, 1)
                pe.wait_ge(s_sgn, 1)
                for dc in range(DC):
                    bank = ps_f[:, dc, :].bitcast(fp16)
                    for hc in range(HC):
                        last = nc.tensor.transpose(bank[:, hc * P:(hc + 1) * P],
                                                   w1_sgn[:, hc, dc * P:(dc + 1) * P], ident16[:, :])
                last.then_inc(s_setup_pe, 1)
                pe.wait_ge(s_sgn, 2)
                for half in range(2):
                    bank = ps_o[:, half, :].bitcast(fp16)
                    for h4 in range(HC // 2):
                        for dc in range(DC):
                            hc = half * (HC // 2) + h4
                            last = nc.tensor.transpose(bank[:, h4 * D + dc * P:h4 * D + (dc + 1) * P],
                                                       w2_sgn[:, dc, hc * P:(hc + 1) * P], ident16[:, :])
                last.then_inc(s_setup_pe, 1)
                pe.wait_ge(s_setup_v, 2)
                for dc in range(DC):
                    last = nc.tensor.matmul(ps_s[:, dc * P:(dc + 1) * P], alpha2_sq[:, dc, :], ident[:, :],
                                            start=True, stop=True)
                last.then_inc(s_setup_pe, 1)

            def prologue():
                pe.wait_ge(s_setup_ev, 3)
                TX(0, 0, 0, True)
                R(0, True)
                TX(1, 0, 1)
                other_weights()
                pe.wait_ge(s_ready, 1)
                pe.wait_ge(s_wcopy, 4)
                O(0, 0)
                R(1, False)
                TX(2, 0, 2)
                T1(0, True)
                O(1, 1)

            def step(i, b, j, left):
                F1(i)
                if left > 2:
                    R(i + 2, False)
                F2(i, left)
                if left > 1:
                    T1(i + 1, False)
                if left > 3:
                    TX(i + 3, b + (j + 3) // CPB, (j + 3) % CPB)
                if left > 2:
                    O(i + 2, 2)

            steps_of(pe, prologue, step)

        @block.scalar
        def _(act):
            def xh(c, j):
                act.wait_ge(s_tx, c + 1)
                act.wait_ge(s_xscl, c + 1)
                nc.scalar.activation(x_hi[:, :, :], ps_r[:, 0:DC, :], ACT.Copy,
                                     scale=x_scl[:, j, 0:1]).then_inc(s_xh, 1)

            def rk(c, j):
                for ec in range(DC):
                    act.wait_ge(s_proj, 6 * c + 3 * ec + 1)
                    nc.scalar.activation(r_tanh[:, ec, :], ps_r[:, 0, :], ACT.Tanh,
                                         scale=x_scl[:, j, 2:3]).then_inc(s_rk, 1)
                    act.wait_ge(s_proj, 6 * c + 3 * ec + 2)
                    nc.scalar.activation(k_sb[:, ec, :], ps_r[:, 1, :], ACT.Copy,
                                         scale=x_scl[:, j, 3:4]).then_inc(s_rk, 1)

            def ysq(c):
                for ec in range(DC):
                    act.wait_ge(s_y, 2 * c + ec + 1)
                    nc.scalar.activation(y_sq[:, ec, :], y[:, ec, :], ACT.Square).then_inc(s_ysq, 1)

            def x1h(c):
                act.wait_ge(s_t1, c + 1)
                nc.scalar.activation(x1_hi[:, :, :], ps_f[:, :, :], ACT.Copy, scale=X1S).then_inc(s_x1h, 1)

            def gelu(c):
                for hc in range(HC):
                    act.wait_ge(s_f1, HC * c + hc + 1)
                    if hc >= NHF:
                        act.wait_ge(s_hl, HC * c + hc - NHF + 1)
                    nc.scalar.activation(hid[:, hc % NHF, :], ps_f[:, hc % 2, :], ACT.Gelu,
                                         bias=b1c[:, hc:hc + 1],
                                         scale=f1_scale[:, hc:hc + 1]).then_inc(s_gelu, 1)

            act.dma_start(lnw_c[:, :], ln_w.rearrange("(c p) -> p c", p=P),
                          allow_slow_non_contiguous=True).then_inc(s_small_in, 16)
            act.dma_start(dec_c[:, 0, :], decay.rearrange("(c p) -> p c", p=P),
                          allow_slow_non_contiguous=True).then_inc(s_small_in, 16)
            act.dma_start(b1c[:, :], b1.rearrange("(c p) -> p c", p=P),
                          allow_slow_non_contiguous=True).then_inc(s_small_in, 16)
            act.dma_start(b2r[:, :], b2.rearrange("(a d) -> a d", a=1).to_broadcast([P, D])).then_inc(s_small_in, 16)
            act.wait_ge(s_small_in, 64)
            nc.scalar.activation(dec_c[:, 1, :], dec_c[:, 0, :], ACT.Sigmoid).then_inc(s_setup_a, 1)
            act.wait_ge(s_setup_v, 1)
            nc.scalar.activation(dec_c[:, 2, :], dec_c[:, 1, :], ACT.Ln).then_inc(s_setup_a, 1)
            act.wait_ge(s_setup_a, 2)
            act.wait_ge(s_const, 1)
            for dc in range(DC):
                nc.scalar.activation(clip_g[:, dc, :], steps[:, :], ACT.Exp, bias=log_clip[:, :],
                                     scale=dec_c[:, 2, dc:dc + 1]).then_inc(s_setup_a, 1)

            def wcopies():
                act.wait_ge(s_setup_pe, 5)
                for dc in range(DC):
                    nc.scalar.activation(w1T[:, dc, :], ps_f[:, dc, :].bitcast(fp16), ACT.Copy).then_inc(s_wcopy, 1)
                act.wait_ge(s_setup_pe, 6)
                for half in range(2):
                    dst = w2T[:, half * 4:half * 4 + 4, :].rearrange("p a d -> p (a d)")
                    nc.scalar.activation(dst, ps_o[:, half, :].bitcast(fp16), ACT.Copy).then_inc(s_wcopy, 1)

            def prologue():
                xh(0, 0)
                rk(0, 0)
                wcopies()
                ysq(0)
                xh(1, 1)
                rk(1, 1)
                ysq(1)
                xh(2, 2)
                x1h(0)

            def step(i, b, j, left):
                gelu(i)
                if left > 2:
                    rk(i + 2, (j + 2) % CPB)
                    ysq(i + 2)
                if left > 1:
                    x1h(i + 1)
                if left > 3:
                    xh(i + 3, (j + 3) % CPB)

            steps_of(act, prologue, step)

        @block.vector
        def _(dve):
            def xmax(c, b, j):
                dve.wait_ge(s_x_in[j], 16 * b + 16)
                nc.vector.tensor_reduce(x_max[:, j, 0:1], x_in[j][:, :, :], AX.XY, ALU.max,
                                        apply_absolute_value=True).then_inc(s_xmax, 1)

            def xl(c, j):
                dve.wait_ge(s_xh, c + 1)
                nc.vector.scalar_tensor_tensor(out=x_lo[:, :, :], in0=ps_r[:, 0:DC, :], scalar=x_scl[:, j, 0:1],
                                               in1=x_hi[:, :, :], op0=ALU.mult,
                                               op1=ALU.subtract).then_inc(s_xl, 1)

            def kvs(c, j):
                for ec in range(DC):
                    dve.wait_ge(s_proj, 6 * c + 3 * ec + 3)
                    dve.wait_ge(s_rk, 4 * c + 2 * ec + 2)
                    nc.vector.scalar_tensor_tensor(out=kv[:, ec, :], in0=ps_r[:, 2, :], scalar=x_scl[:, j, 4:5],
                                                   in1=k_sb[:, ec, :], op0=ALU.mult,
                                                   op1=ALU.mult).then_inc(s_kv, 1)

            def scans(c, j):
                for ec in range(DC):
                    dve.wait_ge(s_kvg, 2 * c + ec + 1)
                    first = state[(j + 1) % 2][:, ec, CH - 1:CH] if j % CPB else 0.0
                    nc.vector.tensor_tensor_scan(state[j % 2][:, ec, :], decay_f[:, ec, :], kvg[:, ec, :], first,
                                                 ALU.mult, ALU.add).then_inc(s_scan, 1)
                for ec in range(DC):
                    dve.wait_ge(s_scan, 2 * c + ec + 1)
                    nc.vector.scalar_tensor_tensor(out=y[:, ec, :], in0=r_tanh[:, ec, :], scalar=1.0,
                                                   in1=state[j % 2][:, ec, :], op0=ALU.add,
                                                   op1=ALU.mult).then_inc(s_y, 1)

            def mean_sq(c):
                dve.wait_ge(s_o, c + 1)
                nc.vector.tensor_scalar(ms[:, :], ps_s[:, 0:TT], 1.0 / D, 4.0 * EPS_RMS, ALU.mult,
                                        ALU.add).then_inc(s_ms, 1)

            def residual1(c, j):
                dve.wait_ge(s_rms, c + 1)
                for tt in range(TT):
                    nc.vector.scalar_tensor_tensor(out=u[:, tt, :], in0=o_tok[:, tt, :], scalar=rms[:, tt:tt + 1],
                                                   in1=x_in[j][:, tt, :], op0=ALU.mult,
                                                   op1=ALU.add).then_inc(s_u, 1)
                for tt in range(TT):
                    dve.wait_ge(s_u, TT * c + tt + 1)
                    nc.vector.bn_stats(u_st[:, tt, :], u[:, tt, :]).then_inc(s_ust, 1)
                dve.wait_ge(s_ust, TT * c + TT)
                stand_alone(dve)
                for tt in range(TT):
                    nc.vector.bn_aggr(u_mv[:, tt, :], u_st[:, tt, :]).then_inc(s_umv, 1)

            def norm1(c):
                dve.wait_ge(s_urstd, c + 1)
                for tt in range(TT):
                    nc.vector.tensor_scalar(x1[:, tt, :], u[:, tt, :], u_mv[:, tt, 0:1], u_rstd[:, tt:tt + 1],
                                            ALU.subtract, ALU.mult).then_inc(s_x1, 1)

            def x1l(c):
                dve.wait_ge(s_x1h, c + 1)
                nc.vector.scalar_tensor_tensor(out=x1_lo[:, :, :], in0=ps_f[:, :, :], scalar=X1S,
                                               in1=x1_hi[:, :, :], op0=ALU.mult,
                                               op1=ALU.subtract).then_inc(s_x1l, 1)

            def hl(c, hcs):
                for hc in hcs:
                    dve.wait_ge(s_hh, HC * c + hc + 1)
                    nc.vector.scalar_tensor_tensor(out=hid_lo[:, hc, :], in0=hid[:, hc % NHF, :],
                                                   scalar=hid_scale[:, :], in1=hid_hi[:, hc, :], op0=ALU.mult,
                                                   op1=ALU.subtract).then_inc(s_hl, 1)

            def zmul(c, j):
                for half in range(2):
                    dve.wait_ge(s_f2, 2 * c + half + 1)
                    nc.vector.tensor_tensor(z[j % 2][:, 2 * half:2 * half + 2, :], o_tok[:, 2 * half:2 * half + 2, :],
                                            alpha2r[:, :].unsqueeze(1).to_broadcast([P, 2, D]),
                                            ALU.mult).then_inc(s_zmul, 1)

            def zstats(c, j):
                for tt in range(TT):
                    dve.wait_ge(s_zadd, 2 * c + tt // 2 + 1)
                    nc.vector.bn_stats(z_st[:, tt, :], z[j % 2][:, tt, :]).then_inc(s_zst, 1)
                dve.wait_ge(s_zst, TT * c + TT)
                stand_alone(dve)
                for tt in range(TT):
                    nc.vector.bn_aggr(z_mv[:, tt, :], z_st[:, tt, :]).then_inc(s_zmv, 1)

            def norm2(c, b, j):
                dve.wait_ge(s_zrstd, c + 1)
                dve.wait_ge(s_stored[j % 2], 16 * (2 * b + j // 2) + 16)
                for tt in range(TT):
                    nc.vector.tensor_scalar(z_out[j % 2][:, tt, :], z[j % 2][:, tt, :], z_mv[:, tt, 0:1],
                                            z_rstd[:, tt:tt + 1], ALU.subtract, ALU.mult).then_inc(s_zout, 1)

            chain = sem("dve_setup_chain")
            done = [0]

            def link(ins):
                done[0] += 1
                ins.then_inc(chain, 1)
                dve.wait_ge(chain, done[0])

            xmax(0, 0, 0)
            dve.wait_ge(s_proj_in, 48)
            for n in range(3):
                nc.vector.tensor_reduce(w_max[:, n:n + 1], proj_in[:, n], AX.XY, ALU.max,
                                        apply_absolute_value=True).then_inc(s_wmax, 1)
            dve.wait_ge(s_setup_a, 1)
            dve.wait_ge(s_small_in, 64)
            nc.vector.tensor_scalar_max(dec_c[:, 1, :], dec_c[:, 1, :], CLIP_DEC).then_inc(s_setup_v, 1)
            dve.wait_ge(s_wamax, 1)
            link(nc.vector.tensor_scalar_max(w_max[:, 0:3], w_amax[:, 0:3], TINY))
            link(nc.vector.reciprocal(w_scl[:, 0:3], w_max[:, 0:3]))
            link(nc.vector.tensor_scalar_mul(w_scl[:, 0:3], w_scl[:, 0:3], TOP))
            link(nc.vector.tensor_scalar_mul(w_inv[:, 0:1], w_max[:, 0:1], 0.5 / TOP))
            link(nc.vector.tensor_scalar_mul(w_inv[:, 1:3], w_max[:, 1:3], 1.0 / TOP))
            for n in range(3):
                dve.wait_ge(s_setup_pe, n + 1)
                hi = proj_hi[:, n].rearrange("p c e -> p (c e)")
                link(nc.vector.tensor_scalar(hi, ps_r[:, n, :], w_scl[:, n:n + 1], None, ALU.mult))
                nc.vector.scalar_tensor_tensor(out=proj_lo[:, n].rearrange("p c e -> p (c e)"), in0=ps_r[:, n, :],
                                               scalar=w_scl[:, n:n + 1], in1=hi, op0=ALU.mult,
                                               op1=ALU.subtract).then_inc(s_setup_ev, 1)
            for dc in range(DC):
                nc.vector.tensor_scalar(decay_f[:, dc, :], steps[:, 0:CH], 0.0, dec_c[:, 1, dc:dc + 1],
                                        ALU.mult, ALU.add)
            for dc in range(DC):
                dve.wait_ge(s_setup_a, 3 + dc)
                last = nc.vector.tensor_scalar_min(clip_g[:, dc, :], clip_g[:, dc, :], 1.0)
            link(last)

            def rest_of_setup():
                dve.wait_ge(s_w1_in, 16)
                dve.wait_ge(s_w2_in, 16)
                for src, dst, m in ((w1_in, w1_sgn, HC), (w2_in, w2_sgn, DC)):
                    link(nc.vector.tensor_scalar(dst[:, :, :], src[:, :, :], 0.0, None, ALU.is_lt))
                    nc.vector.scalar_tensor_tensor(out=dst[:, :, :], in0=src[:, :, :], scalar=0.0, in1=dst[:, :, :],
                                                   op0=ALU.is_gt, op1=ALU.subtract).then_inc(s_sgn, 1)
                link(nc.vector.tensor_reduce(alpha1[:, :], w1_in[:, :, :], AX.X, ALU.add, apply_absolute_value=True))
                link(nc.vector.tensor_reduce(alpha2[:, :], w2_in[:, :, :], AX.X, ALU.add, apply_absolute_value=True))
                link(nc.vector.scalar_tensor_tensor(out=hid_bound[:, 0, :], in0=b1c[:, :], scalar=-1.0, in1=b1c[:, :],
                                                    op0=ALU.mult, op1=ALU.max))
                link(nc.vector.tensor_tensor(hid_bound[:, 1, :], hid_bound[:, 0, :], alpha1[:, :], ALU.add))
                nc.vector.tensor_reduce(w_max[:, 3:4], hid_bound[:, 1, :], AX.X, ALU.max).then_inc(s_wmax, 1)
                link(nc.vector.tensor_scalar_mul(f1_scale[:, :], alpha1[:, :], 1.0 / (D * X1S)))
                dve.wait_ge(s_setup_pe, 4)
                for dc in range(DC):
                    link(nc.vector.tensor_scalar(woT[:, dc, :], ps_s[:, dc * D:(dc + 1) * D], lnw_c[:, dc:dc + 1],
                                                 None, ALU.mult))
                dve.wait_ge(s_wamax, 2)
                link(nc.vector.tensor_scalar_max(w_max[:, 3:4], w_amax[:, 3:4], TINY))
                link(nc.vector.reciprocal(w_scl[:, 3:4], w_max[:, 3:4]))
                link(nc.vector.tensor_scalar_mul(hid_scale[:, :], w_scl[:, 3:4], HTOP))
                link(nc.vector.tensor_scalar(alpha2[:, :], alpha2[:, :], w_max[:, 3:4], 1.0 / (H * HTOP), ALU.mult,
                                             ALU.mult))
                for dc in range(DC):
                    last = nc.vector.tensor_scalar(alpha2_sq[:, dc, :], ones_sq[:, :], alpha2[:, dc:dc + 1], None,
                                                   ALU.mult)
                last.then_inc(s_setup_v, 1)
                dve.wait_ge(s_setup_pe, 7)
                nc.vector.tensor_copy(alpha2r[:, :], ps_s[:, 0:D]).then_inc(s_ready, 1)

            def prologue():
                for n in range(1, 4):
                    xmax(n, 0, n)
                xl(0, 0)
                kvs(0, 0)
                rest_of_setup()
                scans(0, 0)
                xl(1, 1)
                mean_sq(0)
                kvs(1, 1)
                residual1(0, 0)
                scans(1, 1)
                norm1(0)
                xl(2, 2)
                x1l(0)
                mean_sq(1)

            def step(i, b, j, left):
                hl(i, (0, 1))
                if left > 1:
                    residual1(i + 1, (j + 1) % CPB)
                hl(i, (2, 3, 4))
                if left > 1:
                    norm1(i + 1)
                hl(i, (5, 6, 7))
                if left > 2:
                    kvs(i + 2, (j + 2) % CPB)
                    scans(i + 2, (j + 2) % CPB)
                zmul(i, j)
                if left > 1:
                    x1l(i + 1)
                if left > 3:
                    xl(i + 3, (j + 3) % CPB)
                zstats(i, j)
                if left > 4:
                    xmax(i + 4, b + 1, j)
                if left > 2:
                    mean_sq(i + 2)
                norm2(i, b, j)

            steps_of(dve, prologue, step)

        @block.gpsimd
        def _(pool):
            def scales(c, j):
                pool.wait_ge(s_xmax, c + 1)
                stand_alone(pool)
                nc.gpsimd.partition_all_reduce(x_max[:, j, 1:2], x_max[:, j, 0:1], P, RMAX).then_inc(s_xamax, 1)
                pool.wait_ge(s_xamax, c + 1)
                stand_alone(pool)
                nc.gpsimd.tensor_scalar(x_scl[:, j, 1:2], x_max[:, j, 1:2], TINY, 1.0 / TOP, ALU.max,
                                        ALU.mult).then_inc(s_xtmp, 1)
                pool.wait_ge(s_xtmp, c + 1)
                nc.gpsimd.tensor_tensor(x_scl[:, j, 0:1], x_scl[:, j, 1:2], neg_one[:, :], ALU.pow)
                nc.gpsimd.tensor_tensor(x_scl[:, j, 2:5], w_inv[:, :],
                                        x_scl[:, j, 1:2].to_broadcast([P, 3]), ALU.mult).then_inc(s_xscl, 1)

            def gate(c, j):
                for ec in range(DC):
                    pool.wait_ge(s_kv, 2 * c + ec + 1)
                    nc.gpsimd.tensor_tensor(kvg[:, ec, :], kv[:, ec, :], clip_g[:, ec, j * CH:(j + 1) * CH],
                                            ALU.mult).then_inc(s_kvg, 1)

            def ysqs(c):
                pool.wait_ge(s_ysq, 2 * c + 2)
                nc.gpsimd.tensor_tensor(y_sqs[:, :], y_sq[:, 0, :], y_sq[:, 1, :], ALU.add).then_inc(s_ysqs, 1)

            def root_rms(c):
                pool.wait_ge(s_ms, c + 1)
                nc.gpsimd.tensor_tensor(rms[:, :], ms[:, :], neg_half[:, :], ALU.pow).then_inc(s_rms, 1)

            def root_u(c):
                pool.wait_ge(s_umv, TT * c + TT)
                stand_alone(pool)
                nc.gpsimd.tensor_scalar(u_ve[:, :], u_mv[:, :, 1], EPS_LN, 1.0, ALU.add, ALU.mult).then_inc(s_uve, 1)
                pool.wait_ge(s_uve, c + 1)
                nc.gpsimd.tensor_tensor(u_rstd[:, :], u_ve[:, :], neg_half[:, :], ALU.pow).then_inc(s_urstd, 1)

            def add_b2(c, j):
                pool.wait_ge(s_x1, TT * c + TT)
                nc.gpsimd.tensor_tensor(x1b[j % 2][:, :, :], x1[:, :, :],
                                        b2r[:, :].unsqueeze(1).to_broadcast([P, TT, D]),
                                        ALU.add).then_inc(s_x1b, 1)

            def hh(c, hcs):
                for hc in hcs:
                    pool.wait_ge(s_gelu, HC * c + hc + 1)
                    stand_alone(pool)
                    nc.gpsimd.tensor_scalar(hid_hi[:, hc, :], hid[:, hc % NHF, :], hid_scale[:, :], 1.0, ALU.mult,
                                            ALU.mult).then_inc(s_hh, 1)

            def zadd(c, j):
                pool.wait_ge(s_x1b, c + 1)
                for half in range(2):
                    pool.wait_ge(s_zmul, 2 * c + half + 1)
                    part = z[j % 2][:, 2 * half:2 * half + 2, :]
                    nc.gpsimd.tensor_tensor(part, part, x1b[j % 2][:, 2 * half:2 * half + 2, :],
                                            ALU.add).then_inc(s_zadd, 1)

            def root_z(c):
                pool.wait_ge(s_zmv, TT * c + TT)
                stand_alone(pool)
                nc.gpsimd.tensor_scalar(z_ve[:, :], z_mv[:, :, 1], EPS_LN, 1.0, ALU.add, ALU.mult).then_inc(s_zve, 1)
                pool.wait_ge(s_zve, c + 1)
                nc.gpsimd.tensor_tensor(z_rstd[:, :], z_ve[:, :], neg_half[:, :], ALU.pow).then_inc(s_zrstd, 1)

            nc.gpsimd.memset(ident[:, :], 0.0).then_inc(s_zeroed, 1)
            nc.gpsimd.memset(ident16[:, :], 0.0).then_inc(s_zeroed, 1)
            nc.gpsimd.memset(ones_col[:, :], 1.0)
            nc.gpsimd.memset(ones_sq[:, :], 1.0)
            nc.gpsimd.memset(neg_half[:, :], -0.5)
            nc.gpsimd.memset(neg_one[:, :], -1.0)
            pool.wait_ge(s_zeroed, 2)
            for m in (ident, ident16):
                nc.gpsimd.affine_select(out=m[:, :], in_=m[:, :], compare_op=ALU.not_equal, fill=1.0, base=0,
                                        pattern=[[-1, P]], channel_multiplier=1).then_inc(s_ident, 1)
            nc.gpsimd.memset(log_clip[:, :], LOG_CLIP)
            nc.gpsimd.iota(steps[:, :], [[1, T]], base=0, channel_multiplier=0,
                           allow_small_or_imprecise_dtypes=True).then_inc(s_const, 1)
            pool.wait_ge(s_wmax, 3)
            nc.gpsimd.partition_all_reduce(w_amax[:, 0:3], w_max[:, 0:3], P, RMAX).then_inc(s_wamax, 1)

            def prologue():
                pool.wait_ge(s_setup_ev, 3)
                for n in range(4):
                    scales(n, n)
                pool.wait_ge(s_wmax, 4)
                nc.gpsimd.partition_all_reduce(w_amax[:, 3:4], w_max[:, 3:4], P, RMAX).then_inc(s_wamax, 1)
                pool.wait_ge(s_ready, 1)
                gate(0, 0)
                ysqs(0)
                root_rms(0)
                gate(1, 1)
                root_u(0)
                ysqs(1)
                add_b2(0, 0)
                root_rms(1)

            def step(i, b, j, left):
                hh(i, (0, 1, 2, 3))
                if left > 1:
                    root_u(i + 1)
                hh(i, (4, 5, 6, 7))
                if left > 1:
                    add_b2(i + 1, j + 1)
                if left > 2:
                    gate(i + 2, (j + 2) % CPB)
                    ysqs(i + 2)
                zadd(i, j)
                root_z(i)
                if left > 4:
                    scales(i + 4, j)
                if left > 2:
                    root_rms(i + 2)

            steps_of(pool, prologue, step)


_INS = ['L0_attn_x', 'L0_attn_Wr', 'L0_attn_Wk', 'L0_attn_Wv', 'L0_attn_Wo', 'L0_attn_decay', 'L0_attn_ln_w',
        'L0_ffn_w1', 'L0_ffn_b1', 'L0_ffn_w2', 'L0_ffn_b2']
_OUTS = [((8, 2048, 256), 'float32')]


def kernel(**inputs):
    import numpy as _np
    import concourse.bacc as _bacc
    from concourse import mybir as _mybir
    from concourse.bass_utils import run_bass_kernel_spmd as _run

    nc = _bacc.Bacc("TRN2", target_bir_lowering=False, num_devices=1)
    arrays, args = {}, []
    for name in _INS:
        a = _np.ascontiguousarray(inputs[name])
        arrays[f"in_{name}_dram"] = a
        args.append(nc.dram_tensor(f"in_{name}_dram", a.shape, _mybir.dt.from_np(a.dtype), kind="ExternalInput").ap())
    for i, (shape, dtype) in enumerate(_OUTS):
        dt = _mybir.dt.from_np(_np.dtype(dtype))
        args.append(nc.dram_tensor(f"out_{i}_dram", shape, dt, kind="ExternalOutput").ap())
    postln_layer_kernel(nc, *args)
    r = _run(nc, [arrays], core_ids=[0])
    got = tuple(r.results[0][f"out_{i}_dram"] for i in range(len(_OUTS)))
    return got[0]
```

```python
import concourse.bass as bass
from concourse import mybir
from contextlib import ExitStack

P = 128


def postln_layer_kernel(nc, x, Wr, Wk, Wv, Wo, decay, ln_w, w1, b1, w2, b2, out):
    fp32, fp16, i32 = mybir.dt.float32, mybir.dt.float16, mybir.dt.int32
    ALU, ACT, AX = mybir.AluOpType, mybir.ActivationFunctionType, mybir.AxisListType
    RMAX = bass.bass_isa.ReduceOp.max

    B, T, D = x.shape
    H = w1.shape[0]
    CH = 512
    CPB = T // CH
    NCH = B * CPB
    TT = CH // P
    DC = D // P
    HC = H // P
    TOP = 16384.0
    X1S = 2048.0
    HTOP = 32768.0
    TINY = 1e-30
    EPS_RMS, EPS_LN = 1e-6, 1e-5
    CLIP_SCALE, LOG_CLIP = 1e-10, 23.025850929940457
    CLIP_DEC = 1e-7

    x_v = x.rearrange("b (c tt p) d -> (b c) p tt d", c=CPB, p=P)
    out_v = out.rearrange("b (c tt p) d -> (b c) p tt d", c=CPB, p=P)

    ctx = ExitStack()
    with ctx:
        def sb(name, shape, dt=fp32):
            return ctx.enter_context(nc.sbuf_tensor(name, shape, dt))

        def sem(name):
            return ctx.enter_context(nc.semaphore(name))

        ident = sb("ident", [P, P])
        ident16 = sb("ident16", [P, P], fp16)
        ones_col = sb("ones_col", [P, 1])
        ones_sq = sb("ones_sq", [P, P])
        proj_hi = sb("proj_hi", [P, 3, DC, D], fp16)
        proj_lo = sb("proj_lo", [P, 3, DC, D], fp16)
        woT = sb("woT", [P, DC, D])
        w1T = sb("w1T", [P, DC, H], fp16)
        w2T = sb("w2T", [P, HC, D], fp16)
        f1_scale = sb("f1_scale", [P, HC])
        b1c = sb("b1c", [P, HC])
        b2r = sb("b2r", [P, D])
        alpha2r = sb("alpha2r", [P, D])
        hid_scale = sb("hid_scale", [P, 1])
        decay_f = sb("decay_f", [P, DC, CH])
        clip_g = sb("clip_g", [P, DC, T])
        w_inv = sb("w_inv", [P, 3])

        proj_in = sb("proj_in", [P, 3, DC, D])
        wo_in = sb("wo_in", [P, DC, D])
        w1_in = sb("w1_in", [P, HC, D])
        w2_in = sb("w2_in", [P, DC, H])
        w1_sgn = sb("w1_sgn", [P, HC, D], fp16)
        w2_sgn = sb("w2_sgn", [P, DC, H], fp16)
        steps = sb("steps", [P, T])
        lnw_c = sb("lnw_c", [P, DC])
        dec_c = sb("dec_c", [P, 3, DC])
        log_clip = sb("log_clip", [P, 1])
        w_max = sb("w_max", [P, 4])
        w_amax = sb("w_amax", [P, 4])
        w_scl = sb("w_scl", [P, 4])
        alpha1 = sb("alpha1", [P, HC])
        alpha2 = sb("alpha2", [P, DC])
        hid_bound = sb("hid_bound", [P, 2, HC])
        alpha2_sq = sb("alpha2_sq", [P, DC, P])

        x_in = [sb(f"x_in{n}", [P, TT, D]) for n in range(CPB)]
        x_max = sb("x_max", [P, CPB, 2])
        x_scl = sb("x_scl", [P, CPB, 5])
        x_hi = sb("x_hi", [P, DC, CH], fp16)
        x_lo = sb("x_lo", [P, DC, CH], fp16)
        r_tanh = sb("r_tanh", [P, DC, CH])
        k_sb = sb("k_sb", [P, DC, CH])
        kv = sb("kv", [P, DC, CH])
        kvg = sb("kvg", [P, DC, CH])
        state = [sb(f"state{n}", [P, DC, CH]) for n in range(2)]
        y = sb("y", [P, DC, CH])
        y_sq = sb("y_sq", [P, DC, CH])
        y_sqs = sb("y_sqs", [P, CH])
        ms = sb("ms", [P, TT])
        rms = sb("rms", [P, TT])
        u = sb("u", [P, TT, D])
        u_st = sb("u_st", [P, TT, 6])
        u_mv = sb("u_mv", [P, TT, 2])
        u_ve = sb("u_ve", [P, TT])
        u_rstd = sb("u_rstd", [P, TT])
        x1 = sb("x1", [P, TT, D])
        x1b = [sb(f"x1b{n}", [P, TT, D]) for n in range(2)]
        x1_hi = sb("x1_hi", [P, DC, CH], fp16)
        x1_lo = sb("x1_lo", [P, DC, CH], fp16)
        hid = sb("hid", [P, HC, CH])
        hid_hi = sb("hid_hi", [P, HC, CH], fp16)
        hid_lo = sb("hid_lo", [P, HC, CH], fp16)
        z = [sb(f"z{n}", [P, TT, D]) for n in range(2)]
        z_st = sb("z_st", [P, TT, 6])
        z_mv = sb("z_mv", [P, TT, 2])
        z_ve = sb("z_ve", [P, TT])
        z_rstd = sb("z_rstd", [P, TT])
        z_out = [sb(f"z_out{n}", [P, TT, D]) for n in range(2)]
        neg_one = sb("neg_one", [P, 1])
        neg_half = sb("neg_half", [P, TT])

        abs_w1 = hid[:, 0:HC // 2, :].rearrange("p a (b d) -> p (a b) d", d=D)
        abs_w2 = hid[:, HC // 2:HC, :].rearrange("p (c a) t -> p c (a t)", c=DC)

        ps_o = ctx.enter_context(nc.psum_tensor("ps_o", [P, 2, CH], fp32))
        ps_f = ctx.enter_context(nc.psum_tensor("ps_f", [P, 2, CH], fp32))
        ps_r = ctx.enter_context(nc.psum_tensor("ps_r", [P, 3, CH], fp32))
        ps_s = ctx.enter_context(nc.psum_tensor("ps_s", [P, CH], fp32))
        f1_bank = [ps_f[:, 0, :], ps_f[:, 1, :], ps_r[:, 2, :]]
        NF = len(f1_bank)
        proj_bank = [ps_o[:, 0, :], ps_o[:, 1, :], ps_f[:, 0, :]]
        o_tok = ps_o[:, :, :].rearrange("p a (b d) -> p (a b) d", d=D)

        s_proj_in, s_wo_in, s_w1_in, s_w2_in = (sem(n) for n in ("proj_in_s", "wo_in_s", "w1_in_s", "w2_in_s"))
        s_small_in = sem("small_in_s")
        s_zeroed, s_ident, s_const = sem("zeroed_s"), sem("ident_s"), sem("const_s")
        s_wmax, s_wamax = sem("wmax_s"), sem("wamax_s")
        s_setup_pe, s_setup_ev, s_setup_v, s_setup_a = (sem(n) for n in ("setup_pe", "setup_ev", "setup_v", "setup_a"))
        s_sgn, s_wcopy, s_ready = sem("sgn_s"), sem("wcopy_s"), sem("weights_ready_s")
        s_winv, s_wscl, s_proj_hi, s_alpha, s_clip = sem("winv_s"), sem("wscl_s"), sem("proj_hi_s"), sem("alpha_s"), sem("clip_s")
        s_passed = [sem("passed_pool_s"), sem("passed_dve_s")]
        s_x_in = [sem(f"x_in_s{n}") for n in range(CPB)]
        s_xmax, s_xscl = sem("xmax_s"), sem("xscl_s")
        s_xamax = sem("xamax_s")
        s_xtmp = sem("xtmp_s")
        s_tx, s_xh, s_xl = sem("tx_s"), sem("xh_s"), sem("xl_s")
        s_proj, s_rk, s_kv, s_kvg = sem("proj_s"), sem("rk_s"), sem("kv_s"), sem("kvg_s")
        s_scan, s_y, s_ysq, s_ysqs = sem("scan_s"), sem("y_s"), sem("ysq_s"), sem("ysqs_s")
        s_o, s_ms, s_rms, s_u = sem("o_s"), sem("ms_s"), sem("rms_s"), sem("u_s")
        s_ust, s_umv, s_uve, s_urstd = sem("ust_s"), sem("umv_s"), sem("uve_s"), sem("urstd_s")
        s_x1, s_x1b, s_t1, s_x1h, s_x1l = sem("x1_s"), sem("x1b_s"), sem("t1_s"), sem("x1h_s"), sem("x1l_s")
        s_f1, s_gelu, s_hh, s_hl = sem("f1_s"), sem("gelu_s"), sem("hh_s"), sem("hl_s")
        s_f2, s_zmul, s_zadd = sem("f2_s"), sem("zmul_s"), sem("zadd_s")
        s_zst, s_zmv, s_zve, s_zrstd, s_zout = sem("zst_s"), sem("zmv_s"), sem("zve_s"), sem("zrstd_s"), sem("zout_s")
        s_stored = [sem(f"stored_s{n}") for n in range(2)]

        def stand_alone(eng):
            eng.sem_inc(s_passed[eng is nc.vector], 1)

        def steps_of(eng, prologue, step):
            prologue()
            with eng.Fori(0, B - 1) as b:
                for j in range(CPB):
                    step(b * CPB + j, b, j, NCH)
            for j in range(CPB):
                step((B - 1) * CPB + j, B - 1, j, CPB - j)

        def tile_groups(left):
            n = HC // 2 if left > 2 else 1
            return [slice(h, h + n) for h in range(0, HC, n)]


        block = ctx.enter_context(nc.Block())

        @block.sync
        def _(sp):
            def load(c, b, j):
                sp.dma_start(x_in[j][:, :, :], x_v[c]).then_inc(s_x_in[j], 16)

            for n in range(2):
                sp.sem_inc(s_stored[n], 16)
            load(0, 0, 0)
            for n, w in enumerate((Wr, Wk, Wv)):
                sp.dma_start(proj_in[:, n], w.rearrange("(c p) d -> p c d", p=P)).then_inc(s_proj_in, 16)
            load(1, 0, 1)
            sp.dma_start(wo_in[:, :, :], Wo.rearrange("(c p) d -> p c d", p=P)).then_inc(s_wo_in, 16)
            load(2, 0, 2)
            sp.dma_start(w1_in[:, :, :], w1.rearrange("(c p) d -> p c d", p=P)).then_inc(s_w1_in, 16)
            sp.dma_start(w2_in[:, :, :], w2.rearrange("(c p) h -> p c h", p=P)).then_inc(s_w2_in, 16)
            load(3, 0, 3)

            def step(i, b, j, left):
                if left > 4:
                    sp.wait_ge(s_u, TT * i + TT)
                    load(i + 4, b + 1, j)
                sp.wait_ge(s_zout, TT * i + TT)
                sp.dma_start(out_v[i], z_out[j % 2][:, :, :]).then_inc(s_stored[j % 2], 16)

            steps_of(sp, lambda: None, step)
            for n in range(2):
                sp.wait_ge(s_stored[n], 16 + 16 * NCH // 2)

        @block.tensor
        def _(pe):
            def transposes(dst, src, c):
                for dc in range(DC):
                    for tt in range(TT):
                        last = nc.tensor.transpose(dst[:, dc, tt * P:(tt + 1) * P],
                                                   src[:, tt, dc * P:(dc + 1) * P], ident[:, :])
                return last

            def TX(c, b, j, first=False):
                if not first:
                    pe.wait_ge(s_rk, 4 * c)
                pe.wait_ge(s_x_in[j], 16 * b + 16)
                transposes(ps_r, x_in[j], c).then_inc(s_tx, 1)

            def R(c, first, looped=True):
                pe.wait_ge(s_xh, c + 1)
                pe.wait_ge(s_xl, c + 1)
                for ec in range(DC):
                    for m in range(3):
                        if m < 2 and ec:
                            pe.wait_ge(s_rk, 4 * c + m + 1)
                        if m == 2 and (ec or not first):
                            pe.wait_ge(s_kv, 2 * c + ec)
                        if m == 2 and not ec and looped:
                            pe.wait_ge(s_gelu, HC * c - 2 * HC + 6)
                        if first and not ec:
                            pe.wait_ge(s_setup_ev, m + 1)
                        n = 0
                        for w, xx in ((proj_hi, x_hi), (proj_hi, x_lo), (proj_lo, x_hi)):
                            for dc in range(DC):
                                last = nc.tensor.matmul(ps_r[:, m, :], w[:, m, dc, ec * P:(ec + 1) * P],
                                                        xx[:, dc, :], start=(n == 0), stop=(n == 3 * DC - 1))
                                n += 1
                        last.then_inc(s_proj, 1)

            def O(c, k):
                pe.wait_ge(s_y, 2 * c + 2)
                if k >= 2:
                    pe.wait_ge(s_zmul, 2 * c - 2)
                elif k == 1:
                    pe.wait_ge(s_u, TT)
                for tt in range(TT):
                    for dc in range(DC):
                        nc.tensor.matmul(o_tok[:, tt, :], y[:, dc, tt * P:(tt + 1) * P], woT[:, dc, :],
                                         start=(dc == 0), stop=(dc == DC - 1))
                pe.wait_ge(s_ysqs, c + 1)
                if k:
                    pe.wait_ge(s_ms, c)
                for tt in range(TT):
                    last = nc.tensor.matmul(ps_s[:, tt:tt + 1], y_sqs[:, tt * P:(tt + 1) * P], ones_col[:, :],
                                            start=True, stop=True)
                last.then_inc(s_o, 1)

            def T1(c, first):
                pe.wait_ge(s_x1, TT * c + TT)
                if not first:
                    pe.wait_ge(s_gelu, HC * c)
                transposes(ps_f, x1, c).then_inc(s_t1, 1)

            def F1(c, left, first=False):
                pe.wait_ge(s_x1h, c + 1)
                pe.wait_ge(s_x1l, c + 1)
                for hc in range(HC):
                    if hc == NF - 1:
                        pe.wait_ge(s_kv, DC * c + DC * min(left, 2))
                        if first:
                            pe.wait_ge(s_alpha, HC + DC + 1)
                    if hc >= NF:
                        pe.wait_ge(s_gelu, HC * c + hc - NF + 1)
                    for dc in range(DC):
                        for n, xx in enumerate((x1_hi, x1_lo)):
                            last = nc.tensor.matmul(f1_bank[hc % NF], w1T[:, dc, hc * P:(hc + 1) * P],
                                                    xx[:, dc, :], start=(dc == 0 and n == 0),
                                                    stop=(dc == DC - 1 and n == 1))
                    last.then_inc(s_f1, 1)

            def F2(c, left):
                if left > 1:
                    pe.wait_ge(s_u, TT * c + 2 * TT)
                for tt in range(TT):
                    for hc in range(HC):
                        if tt == 0:
                            pe.wait_ge(s_hl, HC * c + hc + 1)
                        for n, hh in enumerate((hid_hi, hid_lo)):
                            last = nc.tensor.matmul(o_tok[:, tt, :], hh[:, hc, tt * P:(tt + 1) * P],
                                                    w2T[:, hc, :], start=(hc == 0 and n == 0),
                                                    stop=(hc == HC - 1 and n == 1))
                    if tt % 2:
                        last.then_inc(s_f2, 1)

            pe.wait_ge(s_ident, 2)
            TX(0, 0, 0, True)
            pe.wait_ge(s_proj_in, 48)
            for n in range(3):
                for dc in range(DC):
                    for ec in range(DC):
                        last = nc.tensor.transpose(proj_bank[n][:, dc * D + ec * P:dc * D + (ec + 1) * P],
                                                   proj_in[:, n, ec, dc * P:(dc + 1) * P], ident[:, :])
                last.then_inc(s_setup_pe, 1)

            def other_weights():
                pe.wait_ge(s_wo_in, 16)
                for dc in range(DC):
                    for ec in range(DC):
                        last = nc.tensor.transpose(ps_s[:, dc * D + ec * P:dc * D + (ec + 1) * P],
                                                   wo_in[:, ec, dc * P:(dc + 1) * P], ident[:, :])
                last.then_inc(s_setup_pe, 1)
                pe.wait_ge(s_sgn, 1)
                for dc in range(DC):
                    bank = ps_f[:, dc, :].bitcast(fp16)
                    for hc in range(HC):
                        last = nc.tensor.transpose(bank[:, hc * P:(hc + 1) * P],
                                                   w1_sgn[:, hc, dc * P:(dc + 1) * P], ident16[:, :])
                last.then_inc(s_setup_pe, 1)

            def w2_transposes():
                pe.wait_ge(s_sgn, 2)
                pe.wait_ge(s_wcopy, 2)
                for half in range(2):
                    bank = ps_f[:, half, :].bitcast(fp16)
                    for h4 in range(HC // 2):
                        for dc in range(DC):
                            hc = half * (HC // 2) + h4
                            last = nc.tensor.transpose(bank[:, h4 * D + dc * P:h4 * D + (dc + 1) * P],
                                                       w2_sgn[:, dc, hc * P:(hc + 1) * P], ident16[:, :])
                last.then_inc(s_setup_pe, 1)

            def alpha_row():
                pe.wait_ge(s_setup_v, 3)
                pe.wait_ge(s_kv, 2 * DC)
                for dc in range(DC):
                    last = nc.tensor.matmul(ps_r[:, 2, dc * P:(dc + 1) * P], alpha2_sq[:, dc, :], ident[:, :],
                                            start=True, stop=True)
                last.then_inc(s_setup_pe, 1)

            def prologue():
                R(0, True, looped=False)
                TX(1, 0, 1)
                other_weights()
                pe.wait_ge(s_setup_v, 2)
                O(0, 0)
                w2_transposes()
                R(1, False, looped=False)
                TX(2, 0, 2)
                pe.wait_ge(s_wcopy, 4)
                T1(0, True)
                O(1, 1)
                alpha_row()
                F1(0, NCH, first=True)

            def step(i, b, j, left):
                if left > 2:
                    R(i + 2, False)
                F2(i, left)
                if left > 1:
                    T1(i + 1, False)
                if left > 3:
                    TX(i + 3, b + (j + 3) // CPB, (j + 3) % CPB)
                if left > 2:
                    O(i + 2, 2)
                if left > 1:
                    F1(i + 1, left - 1)

            steps_of(pe, prologue, step)

        @block.scalar
        def _(act):
            def xh(c, j):
                act.wait_ge(s_tx, c + 1)
                act.wait_ge(s_xscl, c + 1)
                nc.scalar.activation(x_hi[:, :, :], ps_r[:, 0:DC, :], ACT.Copy,
                                     scale=x_scl[:, j, 0:1]).then_inc(s_xh, 1)

            def rk(c, j, ecs=range(DC)):
                for ec in ecs:
                    act.wait_ge(s_proj, 6 * c + 3 * ec + 1)
                    nc.scalar.activation(r_tanh[:, ec, :], ps_r[:, 0, :], ACT.Tanh,
                                         scale=x_scl[:, j, 2:3]).then_inc(s_rk, 1)
                    act.wait_ge(s_proj, 6 * c + 3 * ec + 2)
                    nc.scalar.activation(k_sb[:, ec, :], ps_r[:, 1, :], ACT.Copy,
                                         scale=x_scl[:, j, 3:4]).then_inc(s_rk, 1)

            def ysq(c):
                for ec in range(DC):
                    act.wait_ge(s_y, 2 * c + ec + 1)
                    nc.scalar.activation(y_sq[:, ec, :], y[:, ec, :], ACT.Square).then_inc(s_ysq, 1)

            def x1h(c):
                act.wait_ge(s_t1, c + 1)
                nc.scalar.activation(x1_hi[:, :, :], ps_f[:, :, :], ACT.Copy, scale=X1S).then_inc(s_x1h, 1)

            def gelu(c):
                for hc in range(HC):
                    act.wait_ge(s_f1, HC * c + hc + 1)
                    nc.scalar.activation(hid[:, hc, :], f1_bank[hc % NF], ACT.Gelu,
                                         bias=b1c[:, hc:hc + 1],
                                         scale=f1_scale[:, hc:hc + 1]).then_inc(s_gelu, 1)

            def hh(c, part):
                act.wait_ge(s_gelu, HC * c + part.stop)
                nc.scalar.activation(hid_hi[:, part, :], hid[:, part, :], ACT.Copy,
                                     scale=hid_scale[:, :]).then_inc(s_hh, part.stop - part.start)

            act.dma_start(lnw_c[:, :], ln_w.rearrange("(c p) -> p c", p=P),
                          allow_slow_non_contiguous=True).then_inc(s_small_in, 16)
            act.dma_start(dec_c[:, 0, :], decay.rearrange("(c p) -> p c", p=P),
                          allow_slow_non_contiguous=True).then_inc(s_small_in, 16)
            act.dma_start(b1c[:, :], b1.rearrange("(c p) -> p c", p=P),
                          allow_slow_non_contiguous=True).then_inc(s_small_in, 16)
            act.dma_start(b2r[:, :], b2.rearrange("(a d) -> a d", a=1).to_broadcast([P, D])).then_inc(s_small_in, 16)
            act.wait_ge(s_small_in, 64)
            nc.scalar.activation(dec_c[:, 1, :], dec_c[:, 0, :], ACT.Sigmoid).then_inc(s_setup_a, 1)
            act.wait_ge(s_setup_v, 1)
            nc.scalar.activation(dec_c[:, 2, :], dec_c[:, 1, :], ACT.Ln).then_inc(s_setup_a, 1)
            for n in range(3):
                act.wait_ge(s_setup_pe, n + 1)
                act.wait_ge(s_wscl, 1)
                nc.scalar.activation(proj_hi[:, n].rearrange("p c e -> p (c e)"), proj_bank[n], ACT.Copy,
                                     scale=w_scl[:, n:n + 1]).then_inc(s_proj_hi, 1)

            def clip_table():
                act.wait_ge(s_setup_a, 2)
                act.wait_ge(s_const, 1)
                for dc in range(DC):
                    nc.scalar.activation(clip_g[:, dc, :], steps[:, :], ACT.Exp, bias=log_clip[:, :],
                                         scale=dec_c[:, 2, dc:dc + 1]).then_inc(s_setup_a, 1)

            def alphas1():
                act.wait_ge(s_w1_in, 16)
                for hc in range(HC):
                    nc.scalar.activation(abs_w1[:, hc, :], w1_in[:, hc, :], ACT.Abs,
                                         accum_out=alpha1[:, hc:hc + 1]).then_inc(s_alpha, 1)

            def alphas2():
                act.wait_ge(s_w2_in, 16)
                for dc in range(DC):
                    nc.scalar.activation(abs_w2[:, dc, :], w2_in[:, dc, :], ACT.Abs,
                                         accum_out=alpha2[:, dc:dc + 1]).then_inc(s_alpha, 1)

            def w1_copies():
                act.wait_ge(s_setup_pe, 5)
                for dc in range(DC):
                    nc.scalar.activation(w1T[:, dc, :], ps_f[:, dc, :].bitcast(fp16), ACT.Copy).then_inc(s_wcopy, 1)

            def w2_copies():
                act.wait_ge(s_setup_pe, 6)
                for half in range(2):
                    dst = w2T[:, half * 4:half * 4 + 4, :].rearrange("p a d -> p (a d)")
                    nc.scalar.activation(dst, ps_f[:, half, :].bitcast(fp16), ACT.Copy).then_inc(s_wcopy, 1)

            def prologue():
                xh(0, 0)
                clip_table()
                rk(0, 0)
                xh(1, 1)
                alphas1()
                w1_copies()
                ysq(0)
                alphas2()
                w2_copies()
                rk(1, 1)
                xh(2, 2)
                x1h(0)
                act.wait_ge(s_ready, 1)
                ysq(1)
                gelu(0)
                act.wait_ge(s_ready, 2)

            def step(i, b, j, left):
                if left > 2:
                    parts = tile_groups(left)
                    hh(i, parts[0])
                    rk(i + 2, (j + 2) % CPB, (0,))
                    hh(i, parts[1])
                    rk(i + 2, (j + 2) % CPB, (1,))
                    ysq(i + 2)
                if left > 1:
                    x1h(i + 1)
                if left > 3:
                    xh(i + 3, (j + 3) % CPB)
                if left > 1:
                    gelu(i + 1)

            steps_of(act, prologue, step)

        @block.vector
        def _(dve):
            def xmax(c, b, j):
                dve.wait_ge(s_x_in[j], 16 * b + 16)
                nc.vector.tensor_reduce(x_max[:, j, 0:1], x_in[j][:, :, :], AX.XY, ALU.max,
                                        apply_absolute_value=True).then_inc(s_xmax, 1)

            def xl(c, j):
                dve.wait_ge(s_xh, c + 1)
                nc.vector.scalar_tensor_tensor(out=x_lo[:, :, :], in0=ps_r[:, 0:DC, :], scalar=x_scl[:, j, 0:1],
                                               in1=x_hi[:, :, :], op0=ALU.mult,
                                               op1=ALU.subtract).then_inc(s_xl, 1)

            def kvs(c, j, ec):
                dve.wait_ge(s_proj, 6 * c + 3 * ec + 3)
                dve.wait_ge(s_rk, 4 * c + 2 * ec + 2)
                nc.vector.scalar_tensor_tensor(out=kv[:, ec, :], in0=ps_r[:, 2, :], scalar=x_scl[:, j, 4:5],
                                               in1=k_sb[:, ec, :], op0=ALU.mult,
                                               op1=ALU.mult).then_inc(s_kv, 1)

            def scans(c, j, ec):
                dve.wait_ge(s_kvg, 2 * c + ec + 1)
                first = state[(j + 1) % 2][:, ec, CH - 1:CH] if j % CPB else 0.0
                nc.vector.tensor_tensor_scan(state[j % 2][:, ec, :], decay_f[:, ec, :], kvg[:, ec, :], first,
                                             ALU.mult, ALU.add).then_inc(s_scan, 1)
                dve.wait_ge(s_scan, 2 * c + ec + 1)
                nc.vector.scalar_tensor_tensor(out=y[:, ec, :], in0=r_tanh[:, ec, :], scalar=1.0,
                                               in1=state[j % 2][:, ec, :], op0=ALU.add,
                                               op1=ALU.mult).then_inc(s_y, 1)

            def mean_sq(c):
                dve.wait_ge(s_o, c + 1)
                nc.vector.tensor_scalar(ms[:, :], ps_s[:, 0:TT], 1.0 / D, 4.0 * EPS_RMS, ALU.mult,
                                        ALU.add).then_inc(s_ms, 1)

            def residual1(c, j):
                dve.wait_ge(s_rms, c + 1)
                for tt in range(TT):
                    nc.vector.scalar_tensor_tensor(out=u[:, tt, :], in0=o_tok[:, tt, :], scalar=rms[:, tt:tt + 1],
                                                   in1=x_in[j][:, tt, :], op0=ALU.mult,
                                                   op1=ALU.add).then_inc(s_u, 1)
                for tt in range(TT):
                    dve.wait_ge(s_u, TT * c + tt + 1)
                    nc.vector.bn_stats(u_st[:, tt, :], u[:, tt, :]).then_inc(s_ust, 1)
                dve.wait_ge(s_ust, TT * c + TT)
                stand_alone(dve)
                for tt in range(TT):
                    nc.vector.bn_aggr(u_mv[:, tt, :], u_st[:, tt, :]).then_inc(s_umv, 1)

            def norm1(c):
                dve.wait_ge(s_urstd, c + 1)
                for tt in range(TT):
                    nc.vector.tensor_scalar(x1[:, tt, :], u[:, tt, :], u_mv[:, tt, 0:1], u_rstd[:, tt:tt + 1],
                                            ALU.subtract, ALU.mult).then_inc(s_x1, 1)

            def x1l(c):
                dve.wait_ge(s_x1h, c + 1)
                nc.vector.scalar_tensor_tensor(out=x1_lo[:, :, :], in0=ps_f[:, :, :], scalar=X1S,
                                               in1=x1_hi[:, :, :], op0=ALU.mult,
                                               op1=ALU.subtract).then_inc(s_x1l, 1)

            def hl(c, part):
                dve.wait_ge(s_hh, HC * c + part.stop)
                nc.vector.scalar_tensor_tensor(out=hid_lo[:, part, :], in0=hid[:, part, :], scalar=hid_scale[:, :],
                                               in1=hid_hi[:, part, :], op0=ALU.mult,
                                               op1=ALU.subtract).then_inc(s_hl, part.stop - part.start)

            def zmul(c, j):
                for half in range(2):
                    dve.wait_ge(s_f2, 2 * c + half + 1)
                    nc.vector.tensor_tensor(z[j % 2][:, 2 * half:2 * half + 2, :], o_tok[:, 2 * half:2 * half + 2, :],
                                            alpha2r[:, :].unsqueeze(1).to_broadcast([P, 2, D]),
                                            ALU.mult).then_inc(s_zmul, 1)

            def zstats(c, j):
                for tt in range(TT):
                    dve.wait_ge(s_zadd, 2 * c + tt // 2 + 1)
                    nc.vector.bn_stats(z_st[:, tt, :], z[j % 2][:, tt, :]).then_inc(s_zst, 1)
                dve.wait_ge(s_zst, TT * c + TT)
                stand_alone(dve)
                for tt in range(TT):
                    nc.vector.bn_aggr(z_mv[:, tt, :], z_st[:, tt, :]).then_inc(s_zmv, 1)

            def norm2(c, b, j):
                dve.wait_ge(s_zrstd, c + 1)
                dve.wait_ge(s_stored[j % 2], 16 * (2 * b + j // 2) + 16)
                for tt in range(TT):
                    nc.vector.tensor_scalar(z_out[j % 2][:, tt, :], z[j % 2][:, tt, :], z_mv[:, tt, 0:1],
                                            z_rstd[:, tt:tt + 1], ALU.subtract, ALU.mult).then_inc(s_zout, 1)

            chain = sem("dve_setup_chain")
            done = [0]

            def link(ins):
                done[0] += 1
                ins.then_inc(chain, 1)
                dve.wait_ge(chain, done[0])

            xmax(0, 0, 0)
            dve.wait_ge(s_proj_in, 48)
            for n in range(3):
                nc.vector.tensor_reduce(w_max[:, n:n + 1], proj_in[:, n], AX.XY, ALU.max,
                                        apply_absolute_value=True).then_inc(s_wmax, 1)
            dve.wait_ge(s_setup_a, 1)
            dve.wait_ge(s_small_in, 64)
            nc.vector.tensor_scalar_max(dec_c[:, 1, :], dec_c[:, 1, :], CLIP_DEC).then_inc(s_setup_v, 1)
            dve.wait_ge(s_wamax, 1)
            link(nc.vector.tensor_scalar_max(w_max[:, 0:3], w_amax[:, 0:3], TINY))
            link(nc.vector.reciprocal(w_scl[:, 0:3], w_max[:, 0:3]))
            nc.vector.tensor_scalar_mul(w_scl[:, 0:3], w_scl[:, 0:3], TOP).then_inc(s_wscl, 1)
            nc.vector.tensor_scalar_mul(w_inv[:, 0:1], w_max[:, 0:1], 0.5 / TOP)
            nc.vector.tensor_scalar_mul(w_inv[:, 1:3], w_max[:, 1:3], 1.0 / TOP).then_inc(s_winv, 1)
            for n in range(3):
                dve.wait_ge(s_proj_hi, n + 1)
                nc.vector.scalar_tensor_tensor(out=proj_lo[:, n].rearrange("p c e -> p (c e)"), in0=proj_bank[n],
                                               scalar=w_scl[:, n:n + 1],
                                               in1=proj_hi[:, n].rearrange("p c e -> p (c e)"), op0=ALU.mult,
                                               op1=ALU.subtract).then_inc(s_setup_ev, 1)
                if n == 0:
                    xl(0, 0)

            def decay_rows():
                dve.wait_ge(s_const, 1)
                for dc in range(DC):
                    nc.vector.tensor_scalar(decay_f[:, dc, :], steps[:, 0:CH], 0.0, dec_c[:, 1, dc:dc + 1],
                                            ALU.mult, ALU.add)

            def wo():
                dve.wait_ge(s_setup_pe, 4)
                for dc in range(DC):
                    last = nc.vector.tensor_scalar(woT[:, dc, :], ps_s[:, dc * D:(dc + 1) * D], lnw_c[:, dc:dc + 1],
                                                   None, ALU.mult)
                last.then_inc(s_setup_v, 1)

            def sign(src, dst, landed):
                dve.wait_ge(landed, 16)
                link(nc.vector.tensor_scalar(dst[:, :, :], src[:, :, :], 0.0, None, ALU.is_lt))
                nc.vector.scalar_tensor_tensor(out=dst[:, :, :], in0=src[:, :, :], scalar=0.0, in1=dst[:, :, :],
                                               op0=ALU.is_gt, op1=ALU.subtract).then_inc(s_sgn, 1)

            def hidden_bound():
                dve.wait_ge(s_alpha, HC + DC)
                link(nc.vector.scalar_tensor_tensor(out=hid_bound[:, 0, :], in0=b1c[:, :], scalar=-1.0,
                                                    in1=b1c[:, :], op0=ALU.mult, op1=ALU.max))
                link(nc.vector.tensor_tensor(hid_bound[:, 1, :], hid_bound[:, 0, :], alpha1[:, :], ALU.add))
                nc.vector.tensor_reduce(w_max[:, 3:4], hid_bound[:, 1, :], AX.X, ALU.max).then_inc(s_wmax, 1)
                nc.vector.tensor_scalar_mul(f1_scale[:, :], alpha1[:, :], 1.0 / (D * X1S)).then_inc(s_ready, 1)

            def hidden_scale():
                dve.wait_ge(s_wamax, 2)
                link(nc.vector.tensor_scalar_max(w_max[:, 3:4], w_amax[:, 3:4], TINY))
                link(nc.vector.reciprocal(w_scl[:, 3:4], w_max[:, 3:4]))
                nc.vector.tensor_scalar_mul(hid_scale[:, :], w_scl[:, 3:4], HTOP).then_inc(s_ready, 1)
                link(nc.vector.tensor_scalar(alpha2[:, :], alpha2[:, :], w_max[:, 3:4], 1.0 / (H * HTOP), ALU.mult,
                                             ALU.mult))
                for dc in range(DC):
                    last = nc.vector.tensor_scalar(alpha2_sq[:, dc, :], ones_sq[:, :], alpha2[:, dc:dc + 1], None,
                                                   ALU.mult)
                last.then_inc(s_setup_v, 1)

            def alpha_rows():
                dve.wait_ge(s_setup_pe, 7)
                nc.vector.tensor_copy(alpha2r[:, :], ps_r[:, 2, 0:D]).then_inc(s_alpha, 1)
                dve.wait_ge(s_alpha, HC + DC + 1)

            def prologue():
                decay_rows()
                xmax(1, 0, 1)
                for dc in range(DC):
                    dve.wait_ge(s_setup_a, 3 + dc)
                    nc.vector.tensor_scalar_min(clip_g[:, dc, :], clip_g[:, dc, :], 1.0).then_inc(s_clip, 1)
                kvs(0, 0, 0)
                sign(w1_in, w1_sgn, s_w1_in)
                kvs(0, 0, 1)
                wo()
                scans(0, 0, 0)
                scans(0, 0, 1)
                xl(1, 1)
                sign(w2_in, w2_sgn, s_w2_in)
                mean_sq(0)
                xmax(2, 0, 2)
                residual1(0, 0)
                kvs(1, 1, 0)
                hidden_bound()
                norm1(0)
                scans(1, 1, 0)
                kvs(1, 1, 1)
                x1l(0)
                scans(1, 1, 1)
                hidden_scale()
                xmax(3, 0, 3)
                xl(2, 2)
                mean_sq(1)
                alpha_rows()

            def step(i, b, j, left):
                if left > 1:
                    residual1(i + 1, (j + 1) % CPB)
                if left > 4:
                    xmax(i + 4, b + 1, j)
                parts = tile_groups(left)
                for part in parts[:-1]:
                    hl(i, part)
                if left > 2:
                    kvs(i + 2, (j + 2) % CPB, 0)
                hl(i, parts[-1])
                if left > 1:
                    norm1(i + 1)
                if left > 2:
                    scans(i + 2, (j + 2) % CPB, 0)
                    kvs(i + 2, (j + 2) % CPB, 1)
                    scans(i + 2, (j + 2) % CPB, 1)
                zmul(i, j)
                if left > 1:
                    x1l(i + 1)
                zstats(i, j)
                if left > 3:
                    xl(i + 3, (j + 3) % CPB)
                if left > 2:
                    mean_sq(i + 2)
                norm2(i, b, j)

            steps_of(dve, prologue, step)

        @block.gpsimd
        def _(pool):
            def scales(c, j):
                pool.wait_ge(s_xmax, c + 1)
                stand_alone(pool)
                nc.gpsimd.partition_all_reduce(x_max[:, j, 1:2], x_max[:, j, 0:1], P, RMAX).then_inc(s_xamax, 1)
                pool.wait_ge(s_xamax, c + 1)
                stand_alone(pool)
                nc.gpsimd.tensor_scalar(x_scl[:, j, 1:2], x_max[:, j, 1:2], TINY, 1.0 / TOP, ALU.max,
                                        ALU.mult).then_inc(s_xtmp, 1)
                pool.wait_ge(s_xtmp, c + 1)
                nc.gpsimd.tensor_tensor(x_scl[:, j, 0:1], x_scl[:, j, 1:2], neg_one[:, :], ALU.pow)
                nc.gpsimd.tensor_tensor(x_scl[:, j, 2:5], w_inv[:, :],
                                        x_scl[:, j, 1:2].to_broadcast([P, 3]), ALU.mult).then_inc(s_xscl, 1)

            def gate(c, j, ecs=range(DC)):
                for ec in ecs:
                    pool.wait_ge(s_kv, 2 * c + ec + 1)
                    nc.gpsimd.tensor_tensor(kvg[:, ec, :], kv[:, ec, :], clip_g[:, ec, j * CH:(j + 1) * CH],
                                            ALU.mult).then_inc(s_kvg, 1)

            def ysqs(c):
                pool.wait_ge(s_ysq, 2 * c + 2)
                nc.gpsimd.tensor_tensor(y_sqs[:, :], y_sq[:, 0, :], y_sq[:, 1, :], ALU.add).then_inc(s_ysqs, 1)

            def root_rms(c):
                pool.wait_ge(s_ms, c + 1)
                nc.gpsimd.tensor_tensor(rms[:, :], ms[:, :], neg_half[:, :], ALU.pow).then_inc(s_rms, 1)

            def root_u(c):
                pool.wait_ge(s_umv, TT * c + TT)
                stand_alone(pool)
                nc.gpsimd.tensor_scalar(u_ve[:, :], u_mv[:, :, 1], EPS_LN, 1.0, ALU.add, ALU.mult).then_inc(s_uve, 1)
                pool.wait_ge(s_uve, c + 1)
                nc.gpsimd.tensor_tensor(u_rstd[:, :], u_ve[:, :], neg_half[:, :], ALU.pow).then_inc(s_urstd, 1)

            def add_b2(c, j):
                pool.wait_ge(s_x1, TT * c + TT)
                nc.gpsimd.tensor_tensor(x1b[j % 2][:, :, :], x1[:, :, :],
                                        b2r[:, :].unsqueeze(1).to_broadcast([P, TT, D]),
                                        ALU.add).then_inc(s_x1b, 1)

            def hh(c, part):
                pool.wait_ge(s_gelu, HC * c + part.stop)
                nc.gpsimd.tensor_scalar(hid_hi[:, part, :], hid[:, part, :], hid_scale[:, :], 1.0, ALU.mult,
                                        ALU.mult).then_inc(s_hh, part.stop - part.start)

            def zadd(c, j):
                pool.wait_ge(s_x1b, c + 1)
                for half in range(2):
                    pool.wait_ge(s_zmul, 2 * c + half + 1)
                    part = z[j % 2][:, 2 * half:2 * half + 2, :]
                    nc.gpsimd.tensor_tensor(part, part, x1b[j % 2][:, 2 * half:2 * half + 2, :],
                                            ALU.add).then_inc(s_zadd, 1)

            def root_z(c):
                pool.wait_ge(s_zmv, TT * c + TT)
                stand_alone(pool)
                nc.gpsimd.tensor_scalar(z_ve[:, :], z_mv[:, :, 1], EPS_LN, 1.0, ALU.add, ALU.mult).then_inc(s_zve, 1)
                pool.wait_ge(s_zve, c + 1)
                nc.gpsimd.tensor_tensor(z_rstd[:, :], z_ve[:, :], neg_half[:, :], ALU.pow).then_inc(s_zrstd, 1)

            nc.gpsimd.memset(ident[:, :], 0.0).then_inc(s_zeroed, 1)
            nc.gpsimd.memset(ident16[:, :], 0.0).then_inc(s_zeroed, 1)
            nc.gpsimd.memset(ones_col[:, :], 1.0)
            nc.gpsimd.memset(ones_sq[:, :], 1.0)
            nc.gpsimd.memset(neg_half[:, :], -0.5)
            nc.gpsimd.memset(neg_one[:, :], -1.0)
            pool.wait_ge(s_zeroed, 2)
            for m in (ident, ident16):
                nc.gpsimd.affine_select(out=m[:, :], in_=m[:, :], compare_op=ALU.not_equal, fill=1.0, base=0,
                                        pattern=[[-1, P]], channel_multiplier=1).then_inc(s_ident, 1)
            nc.gpsimd.memset(log_clip[:, :], LOG_CLIP)
            nc.gpsimd.iota(steps[:, :], [[1, T]], base=0, channel_multiplier=0,
                           allow_small_or_imprecise_dtypes=True).then_inc(s_const, 1)
            pool.wait_ge(s_wmax, 3)
            nc.gpsimd.partition_all_reduce(w_amax[:, 0:3], w_max[:, 0:3], P, RMAX).then_inc(s_wamax, 1)

            def prologue():
                pool.wait_ge(s_winv, 1)
                scales(0, 0)
                scales(1, 1)
                pool.wait_ge(s_clip, DC)
                gate(0, 0)
                ysqs(0)
                scales(2, 2)
                root_rms(0)
                root_u(0)
                gate(1, 1, (0,))
                pool.wait_ge(s_wmax, 4)
                nc.gpsimd.partition_all_reduce(w_amax[:, 3:4], w_max[:, 3:4], P, RMAX).then_inc(s_wamax, 1)
                gate(1, 1, (1,))
                ysqs(1)
                scales(3, 3)
                add_b2(0, 0)
                root_rms(1)

            def step(i, b, j, left):
                parts = tile_groups(left) if left <= 2 else ()
                for part in parts[:4]:
                    hh(i, part)
                if left > 1:
                    root_u(i + 1)
                for part in parts[4:]:
                    hh(i, part)
                if left > 2:
                    gate(i + 2, (j + 2) % CPB, (0,))
                if left > 1:
                    add_b2(i + 1, j + 1)
                if left > 2:
                    gate(i + 2, (j + 2) % CPB, (1,))
                    ysqs(i + 2)
                zadd(i, j)
                if left > 4:
                    scales(i + 4, j)
                root_z(i)
                if left > 2:
                    root_rms(i + 2)

            steps_of(pool, prologue, step)


_INS = ['L0_attn_x', 'L0_attn_Wr', 'L0_attn_Wk', 'L0_attn_Wv', 'L0_attn_Wo', 'L0_attn_decay', 'L0_attn_ln_w',
        'L0_ffn_w1', 'L0_ffn_b1', 'L0_ffn_w2', 'L0_ffn_b2']
_OUTS = [((8, 2048, 256), 'float32')]


def kernel(**inputs):
    import numpy as _np
    import concourse.bacc as _bacc
    from concourse import mybir as _mybir
    from concourse.bass_utils import run_bass_kernel_spmd as _run

    nc = _bacc.Bacc("TRN2", target_bir_lowering=False, num_devices=1)
    arrays, args = {}, []
    for name in _INS:
        a = _np.ascontiguousarray(inputs[name])
        arrays[f"in_{name}_dram"] = a
        args.append(nc.dram_tensor(f"in_{name}_dram", a.shape, _mybir.dt.from_np(a.dtype), kind="ExternalInput").ap())
    for i, (shape, dtype) in enumerate(_OUTS):
        dt = _mybir.dt.from_np(_np.dtype(dtype))
        args.append(nc.dram_tensor(f"out_{i}_dram", shape, dt, kind="ExternalOutput").ap())
    postln_layer_kernel(nc, *args)
    r = _run(nc, [arrays], core_ids=[0])
    got = tuple(r.results[0][f"out_{i}_dram"] for i in range(len(_OUTS)))
    return got[0]
```

```python
import concourse.bass as bass
from concourse import mybir
from contextlib import ExitStack

P = 128


def postln_layer_kernel(nc, x, Wr, Wk, Wv, Wo, decay, ln_w, w1, b1, w2, b2, out):
    fp32, fp16, i32 = mybir.dt.float32, mybir.dt.float16, mybir.dt.int32
    ALU, ACT, AX = mybir.AluOpType, mybir.ActivationFunctionType, mybir.AxisListType
    RMAX = bass.bass_isa.ReduceOp.max

    B, T, D = x.shape
    H = w1.shape[0]
    CH = 512
    CPB = T // CH
    NCH = B * CPB
    TT = CH // P
    DC = D // P
    HC = H // P
    TOP = 16384.0
    X1S = 2048.0
    YTOP = 32768.0
    HTOP = 32768.0
    TINY_ROOT = 1e-15
    TINY = 1e-30
    EPS_RMS, EPS_LN = 1e-6, 1e-5
    CLIP_SCALE, LOG_CLIP = 1e-10, 23.025850929940457
    CLIP_DEC = 1e-7

    x_v = x.rearrange("b (c tt p) d -> (b c) p tt d", c=CPB, p=P)
    out_v = out.rearrange("b (c tt p) d -> (b c) p tt d", c=CPB, p=P)

    ctx = ExitStack()
    with ctx:
        def sb(name, shape, dt=fp32):
            return ctx.enter_context(nc.sbuf_tensor(name, shape, dt))

        def sem(name):
            return ctx.enter_context(nc.semaphore(name))

        ident = sb("ident", [P, P])
        ident16 = sb("ident16", [P, P], fp16)
        ones_col = sb("ones_col", [P, 1])
        ones_sq = sb("ones_sq", [P, P])
        proj_hi = sb("proj_hi", [P, 3, DC, D], fp16)
        proj_lo = sb("proj_lo", [P, 3, DC, D], fp16)
        wo_hi = sb("wo_hi", [P, DC, D], fp16)
        wo_lo = sb("wo_lo", [P, DC, D], fp16)
        wo_inv = sb("wo_inv", [P, 1])
        w1T = sb("w1T", [P, DC, H], fp16)
        w2T = sb("w2T", [P, HC, D], fp16)
        f1_scale = sb("f1_scale", [P, HC])
        b1c = sb("b1c", [P, HC])
        b2r = sb("b2r", [P, D])
        alpha2r = sb("alpha2r", [P, D])
        hid_scale = sb("hid_scale", [P, 1])
        decay_f = sb("decay_f", [P, DC, CH])
        clip_g = sb("clip_g", [P, DC, T])
        w_inv = sb("w_inv", [P, 3])

        proj_in = sb("proj_in", [P, 3, DC, D])
        wo_in = sb("wo_in", [P, DC, D])
        w1_in = sb("w1_in", [P, HC, D])
        w2_in = sb("w2_in", [P, DC, H])
        w1_sgn = sb("w1_sgn", [P, HC, D], fp16)
        w2_sgn = sb("w2_sgn", [P, DC, H], fp16)
        steps = sb("steps", [P, T])
        lnw_c = sb("lnw_c", [P, DC])
        dec_c = sb("dec_c", [P, 3, DC])
        log_clip = sb("log_clip", [P, 1])
        w_max = sb("w_max", [P, 6])
        w_amax = sb("w_amax", [P, 6])
        w_scl = sb("w_scl", [P, 6])
        lnw_scl = sb("lnw_scl", [P, DC])
        alpha1 = sb("alpha1", [P, HC])
        alpha2 = sb("alpha2", [P, DC])
        hid_bound = sb("hid_bound", [P, 2, HC])
        alpha2_sq = sb("alpha2_sq", [P, DC, P])

        x_in = [sb(f"x_in{n}", [P, TT, D]) for n in range(CPB)]
        x_max = sb("x_max", [P, CPB, 2])
        x_scl = sb("x_scl", [P, CPB, 5])
        x_hi = sb("x_hi", [P, DC, CH], fp16)
        x_lo = sb("x_lo", [P, DC, CH], fp16)
        r_tanh = sb("r_tanh", [P, DC, CH])
        k_sb = sb("k_sb", [P, DC, CH])
        kv = sb("kv", [P, DC, CH])
        kvg = sb("kvg", [P, DC, CH])
        state = [sb(f"state{n}", [P, DC, CH]) for n in range(2)]
        y = sb("y", [P, DC, CH])
        y_hi = sb("y_hi", [P, DC, CH], fp16)
        y_lo = sb("y_lo", [P, DC, CH], fp16)
        y_norm = sb("y_norm", [P, 2, DC])
        y_q = sb("y_q", [P, 2])
        y_scl = sb("y_scl", [P, 1])
        y_inv = sb("y_inv", [P, 2])
        y_sq = sb("y_sq", [P, DC, CH])
        y_sqs = sb("y_sqs", [P, CH])
        ms = sb("ms", [P, TT])
        root = sb("root", [P, TT])
        rms = sb("rms", [P, TT])
        u = sb("u", [P, TT, D])
        u_st = sb("u_st", [P, TT, 6])
        u_mv = sb("u_mv", [P, TT, 2])
        u_ve = sb("u_ve", [P, TT])
        u_rstd = sb("u_rstd", [P, TT])
        x1 = sb("x1", [P, TT, D])
        x1b = [sb(f"x1b{n}", [P, TT, D]) for n in range(2)]
        x1_hi = sb("x1_hi", [P, DC, CH], fp16)
        x1_lo = sb("x1_lo", [P, DC, CH], fp16)
        hid = sb("hid", [P, HC, CH])
        hid_hi = sb("hid_hi", [P, HC, CH], fp16)
        hid_lo = sb("hid_lo", [P, HC, CH], fp16)
        z = [sb(f"z{n}", [P, TT, D]) for n in range(2)]
        z_st = sb("z_st", [P, TT, 6])
        z_mv = sb("z_mv", [P, TT, 2])
        z_ve = sb("z_ve", [P, TT])
        z_rstd = sb("z_rstd", [P, TT])
        z_out = [sb(f"z_out{n}", [P, TT, D]) for n in range(2)]
        warm = sb("warm", [P, 1])
        neg_one = sb("neg_one", [P, 1])
        neg_half = sb("neg_half", [P, TT])
        half_one = sb("half_one", [P, 1])

        abs_w1 = hid[:, 0:HC // 2, :].rearrange("p a (b d) -> p (a b) d", d=D)
        abs_w2 = hid[:, HC // 2:HC, :].rearrange("p (c a) t -> p c (a t)", c=DC)

        ps_o = ctx.enter_context(nc.psum_tensor("ps_o", [P, 2, CH], fp32))
        ps_f = ctx.enter_context(nc.psum_tensor("ps_f", [P, 2, CH], fp32))
        ps_r = ctx.enter_context(nc.psum_tensor("ps_r", [P, 3, CH], fp32))
        ps_s = ctx.enter_context(nc.psum_tensor("ps_s", [P, CH], fp32))
        f1_bank = [ps_f[:, 0, :], ps_f[:, 1, :], ps_r[:, 2, :]]
        NF = len(f1_bank)
        proj_bank = [ps_o[:, 0, :], ps_o[:, 1, :], ps_f[:, 0, :]]
        o_tok = ps_o[:, :, :].rearrange("p a (b d) -> p (a b) d", d=D)

        o_last = ps_r[:, 0:2, :].rearrange("p a (b d) -> p (a b) d", d=D)
        f2_last = [ps_o[:, 0, 0:D], ps_o[:, 1, 0:D], ps_r[:, 0, 0:D], ps_r[:, 1, 0:D]]

        s_proj_in = [sem(f"proj_in_s{n}") for n in range(3)]
        s_wo_in, s_w1_in, s_w2_in = (sem(n) for n in ("wo_in_s", "w1_in_s", "w2_in_s"))
        s_small_in = sem("small_in_s")
        s_zeroed, s_ident, s_const = sem("zeroed_s"), sem("ident_s"), sem("const_s")
        s_wmax, s_wamax = sem("wmax_s"), sem("wamax_s")
        s_setup_pe, s_setup_ev, s_setup_v, s_setup_a = (sem(n) for n in ("setup_pe", "setup_ev", "setup_v", "setup_a"))
        s_sgn, s_wcopy, s_ready = sem("sgn_s"), sem("wcopy_s"), sem("weights_ready_s")
        s_winv, s_wscl, s_proj_hi, s_alpha, s_clip = sem("winv_s"), sem("wscl_s"), sem("proj_hi_s"), sem("alpha_s"), sem("clip_s")
        s_lnw, s_wo_hi = sem("lnw_s"), sem("wo_hi_s")
        s_passed = [sem("passed_pool_s"), sem("passed_dve_s")]
        s_x_in = [sem(f"x_in_s{n}") for n in range(CPB)]
        s_xmax, s_xscl, s_xun = sem("xmax_s"), sem("xscl_s"), sem("xun_s")
        s_xamax = sem("xamax_s")
        s_xtmp = sem("xtmp_s")
        s_tx, s_xh, s_xl = sem("tx_s"), sem("xh_s"), sem("xl_s")
        s_proj, s_rk, s_kv, s_kvg = sem("proj_s"), sem("rk_s"), sem("kv_s"), sem("kvg_s")
        s_scan, s_y, s_ysq, s_ysqs = sem("scan_s"), sem("y_s"), sem("ysq_s"), sem("ysqs_s")
        s_ynorm, s_yq, s_yq2, s_yscl, s_yinv, s_yinv2, s_yh, s_yl = (sem(n) for n in (
            "ynorm_s", "yq_s", "yq2_s", "yscl_s", "yinv_s", "yinv2_s", "yh_s", "yl_s"))
        s_sums, s_root = sem("sums_s"), sem("root_s")
        s_o, s_ms, s_rms, s_u = sem("o_s"), sem("ms_s"), sem("rms_s"), sem("u_s")
        s_ust, s_umv, s_uve, s_urstd = sem("ust_s"), sem("umv_s"), sem("uve_s"), sem("urstd_s")
        s_x1, s_x1b, s_t1, s_x1h, s_x1l = sem("x1_s"), sem("x1b_s"), sem("t1_s"), sem("x1h_s"), sem("x1l_s")
        s_hh_odd = sem("hh_odd_s")
        s_zadd_last = sem("zadd_last_s")
        s_f1, s_gelu, s_hh, s_hl = sem("f1_s"), sem("gelu_s"), sem("hh_s"), sem("hl_s")
        s_f2, s_zmul, s_zadd = sem("f2_s"), sem("zmul_s"), sem("zadd_s")
        s_zst, s_zmv, s_zve, s_zrstd, s_zout = sem("zst_s"), sem("zmv_s"), sem("zve_s"), sem("zrstd_s"), sem("zout_s")
        s_stored = [sem(f"stored_s{n}") for n in range(2)]

        def stand_alone(eng):
            eng.sem_inc(s_passed[eng is nc.vector], 1)

        def steps_of(eng, prologue, step):
            prologue()
            with eng.Fori(0, B - 1) as b:
                for j in range(CPB):
                    step(b * CPB + j, b, j, NCH)
            for j in range(CPB):
                step((B - 1) * CPB + j, B - 1, j, CPB - j)

        def tile_groups(left):
            n = HC // 2 if left > 2 else 1
            return [slice(h, h + n) for h in range(0, HC, n)]


        block = ctx.enter_context(nc.Block())

        @block.sync
        def _(sp):
            def load(c, b, j):
                sp.dma_start(x_in[j][:, :, :], x_v[c]).then_inc(s_x_in[j], 16)

            for n in range(2):
                sp.sem_inc(s_stored[n], 16)
            load(0, 0, 0)
            for n, w in enumerate((Wr, Wk, Wv)):
                sp.dma_start(proj_in[:, n], w.rearrange("(c p) d -> p c d", p=P)).then_inc(s_proj_in[n], 16)
            load(1, 0, 1)
            sp.dma_start(wo_in[:, :, :], Wo.rearrange("(c p) d -> p c d", p=P)).then_inc(s_wo_in, 16)
            sp.dma_start(w1_in[:, :, :], w1.rearrange("(c p) d -> p c d", p=P)).then_inc(s_w1_in, 16)
            sp.dma_start(w2_in[:, :, :], w2.rearrange("(c p) h -> p c h", p=P)).then_inc(s_w2_in, 16)
            load(2, 0, 2)
            load(3, 0, 3)

            def step(i, b, j, left):
                if left > 4:
                    sp.wait_ge(s_u, TT * i + TT)
                    load(i + 4, b + 1, j)
                sp.wait_ge(s_zout, TT * i + TT)
                sp.dma_start(out_v[i], z_out[j % 2][:, :, :]).then_inc(s_stored[j % 2], 16)

            steps_of(sp, lambda: None, step)
            for n in range(2):
                sp.wait_ge(s_stored[n], 16 + 16 * NCH // 2)

        @block.tensor
        def _(pe):
            def transposes(dst, src, c):
                for dc in range(DC):
                    for tt in range(TT):
                        last = nc.tensor.transpose(dst[:, dc, tt * P:(tt + 1) * P],
                                                   src[:, tt, dc * P:(dc + 1) * P], ident[:, :])
                return last

            def TX(c, b, j, first=False):
                if not first:
                    pe.wait_ge(s_rk, 4 * c)
                pe.wait_ge(s_x_in[j], 16 * b + 16)
                transposes(ps_r, x_in[j], c).then_inc(s_tx, 1)

            def R(c, first, looped=True, ecs=range(DC)):
                pe.wait_ge(s_xh, c + 1)
                pe.wait_ge(s_xl, c + 1)
                for ec in ecs:
                    for m in range(3):
                        if m < 2 and ec:
                            pe.wait_ge(s_rk, 4 * c + m + 1)
                        if m == 2 and (ec or not first):
                            pe.wait_ge(s_kv, 2 * c + ec)
                        if m == 2 and not ec and looped:
                            pe.wait_ge(s_gelu, HC * c - 2 * HC + 6)
                        if first and not ec:
                            pe.wait_ge(s_setup_ev, m + 1)
                        n = 0
                        for w, xx in ((proj_hi, x_hi), (proj_hi, x_lo), (proj_lo, x_hi)):
                            for dc in range(DC):
                                last = nc.tensor.matmul(ps_r[:, m, :], w[:, m, dc, ec * P:(ec + 1) * P],
                                                        xx[:, dc, :], start=(n == 0), stop=(n == 3 * DC - 1))
                                n += 1
                        last.then_inc(s_proj, 1)

            def O(c, k, last_chunk=False):
                dst = o_last if last_chunk else o_tok
                pe.wait_ge(s_ysqs, c + 1)
                if k:
                    pe.wait_ge(s_ms, c)
                if k == 1:
                    pe.wait_ge(s_alpha, HC + DC + 1)
                for tt in range(TT):
                    last = nc.tensor.matmul(ps_s[:, tt:tt + 1], y_sqs[:, tt * P:(tt + 1) * P], ones_col[:, :],
                                            start=True, stop=True)
                last.then_inc(s_sums, 1)
                pe.wait_ge(s_yh, c + 1)
                pe.wait_ge(s_yl, c + 1)
                if k == 0:
                    pe.wait_ge(s_wcopy, 2)
                if k >= 2 and not last_chunk:
                    pe.wait_ge(s_zmul, 2 * c - 2)
                elif k == 1:
                    pe.wait_ge(s_u, TT)
                for tt in range(TT):
                    n = 0
                    for dc in range(DC):
                        for yy, w in ((y_hi, wo_hi), (y_hi, wo_lo), (y_lo, wo_hi)):
                            last = nc.tensor.matmul(dst[:, tt, :], yy[:, dc, tt * P:(tt + 1) * P], w[:, dc, :],
                                                    start=(n == 0), stop=(n == 3 * DC - 1))
                            n += 1
                last.then_inc(s_o, 1)

            def T1(c, first):
                pe.wait_ge(s_x1, TT * c + TT)
                if not first:
                    pe.wait_ge(s_gelu, HC * c)
                transposes(ps_f, x1, c).then_inc(s_t1, 1)

            def F1(c, left, tiles=range(HC)):
                pe.wait_ge(s_x1h, c + 1)
                pe.wait_ge(s_x1l, c + 1)
                for hc in tiles:
                    if hc == NF - 1:
                        pe.wait_ge(s_kv, DC * c + DC * min(left, 2))
                    if hc >= NF:
                        pe.wait_ge(s_gelu, HC * c + hc - NF + 1)
                    for dc in range(DC):
                        for n, xx in enumerate((x1_hi, x1_lo)):
                            last = nc.tensor.matmul(f1_bank[hc % NF], w1T[:, dc, hc * P:(hc + 1) * P],
                                                    xx[:, dc, :], start=(dc == 0 and n == 0),
                                                    stop=(dc == DC - 1 and n == 1))
                    last.then_inc(s_f1, 1)

            def F2_last(c):
                pe.wait_ge(s_u, TT * c + TT)
                pe.wait_ge(s_zmul, 2 * c)
                for hc in range(HC):
                    pe.wait_ge(s_hl, HC * c + hc + 1)
                    for tt in range(TT):
                        for n, hh in enumerate((hid_hi, hid_lo)):
                            last = nc.tensor.matmul(f2_last[tt], hh[:, hc, tt * P:(tt + 1) * P],
                                                    w2T[:, hc, :], start=(hc == 0 and n == 0),
                                                    stop=(hc == HC - 1 and n == 1))
                        if hc == HC - 1 and tt % 2:
                            last.then_inc(s_f2, 1)

            def F2(c, left):
                if left > 2:
                    pe.wait_ge(s_u, TT * c + 2 * TT)
                else:
                    pe.wait_ge(s_zmul, 2 * c)
                for tt in range(TT):
                    if tt == TT - 1 and left > 1:
                        T1(c + 1, False)
                    for hc in range(HC):
                        if tt == 0:
                            pe.wait_ge(s_hl, HC * c + hc + 1)
                        for n, hh in enumerate((hid_hi, hid_lo)):
                            last = nc.tensor.matmul(o_tok[:, tt, :], hh[:, hc, tt * P:(tt + 1) * P],
                                                    w2T[:, hc, :], start=(hc == 0 and n == 0),
                                                    stop=(hc == HC - 1 and n == 1))
                    if tt % 2:
                        last.then_inc(s_f2, 1)

            pe.wait_ge(s_ident, 2)
            TX(0, 0, 0, True)
            for n in range(3):
                pe.wait_ge(s_proj_in[n], 16)
                for dc in range(DC):
                    for ec in range(DC):
                        last = nc.tensor.transpose(proj_bank[n][:, dc * D + ec * P:dc * D + (ec + 1) * P],
                                                   proj_in[:, n, ec, dc * P:(dc + 1) * P], ident[:, :])
                last.then_inc(s_setup_pe, 1)

            def other_weights():
                pe.wait_ge(s_wo_in, 16)
                for dc in range(DC):
                    for ec in range(DC):
                        last = nc.tensor.transpose(ps_s[:, dc * D + ec * P:dc * D + (ec + 1) * P],
                                                   wo_in[:, ec, dc * P:(dc + 1) * P], ident[:, :])
                last.then_inc(s_setup_pe, 1)
                pe.wait_ge(s_sgn, 1)
                for dc in range(DC):
                    bank = ps_o[:, dc, :].bitcast(fp16)
                    for hc in range(HC):
                        last = nc.tensor.transpose(bank[:, hc * P:(hc + 1) * P],
                                                   w1_sgn[:, hc, dc * P:(dc + 1) * P], ident16[:, :])
                last.then_inc(s_setup_pe, 1)

            def w2_transposes():
                pe.wait_ge(s_sgn, 2)
                for half in range(2):
                    bank = ps_f[:, half, :].bitcast(fp16)
                    for h4 in range(HC // 2):
                        for dc in range(DC):
                            hc = half * (HC // 2) + h4
                            last = nc.tensor.transpose(bank[:, h4 * D + dc * P:h4 * D + (dc + 1) * P],
                                                       w2_sgn[:, dc, hc * P:(hc + 1) * P], ident16[:, :])
                last.then_inc(s_setup_pe, 1)

            def alpha_row():
                pe.wait_ge(s_setup_v, 3)
                pe.wait_ge(s_ms, 1)
                for dc in range(DC):
                    last = nc.tensor.matmul(ps_s[:, dc * P:(dc + 1) * P], alpha2_sq[:, dc, :], ident[:, :],
                                            start=True, stop=True)
                last.then_inc(s_setup_pe, 1)

            def prologue():
                R(0, True, looped=False)
                TX(1, 0, 1)
                other_weights()
                R(1, False, looped=False, ecs=(0,))
                pe.wait_ge(s_setup_v, 2)
                O(0, 0)
                w2_transposes()
                R(1, False, looped=False, ecs=(1,))
                TX(2, 0, 2)
                pe.wait_ge(s_wcopy, 4)
                T1(0, True)
                F1(0, NCH, range(NF))
                alpha_row()
                F1(0, NCH, range(NF, HC))
                O(1, 1)

            def step(i, b, j, left):
                if left > 2:
                    R(i + 2, False)
                if left > 1:
                    F2(i, left)
                else:
                    F2_last(i)
                if left > 3:
                    TX(i + 3, b + (j + 3) // CPB, (j + 3) % CPB)
                if left == 3:
                    F1(i + 1, left - 1, range(HC // 2))
                    O(i + 2, 2, last_chunk=True)
                    F1(i + 1, left - 1, range(HC // 2, HC))
                elif left > 1:
                    F1(i + 1, left - 1)
                if left > 3:
                    O(i + 2, 2)

            steps_of(pe, prologue, step)

        @block.scalar
        def _(act):
            def xh(c, j):
                act.wait_ge(s_tx, c + 1)
                act.wait_ge(s_xscl, c + 1)
                nc.scalar.activation(x_hi[:, :, :], ps_r[:, 0:DC, :], ACT.Copy,
                                     scale=x_scl[:, j, 0:1]).then_inc(s_xh, 1)

            def rk(c, j, ecs=range(DC)):
                act.wait_ge(s_xun, c + 1)
                for ec in ecs:
                    act.wait_ge(s_proj, 6 * c + 3 * ec + 1)
                    nc.scalar.activation(r_tanh[:, ec, :], ps_r[:, 0, :], ACT.Tanh,
                                         scale=x_scl[:, j, 2:3]).then_inc(s_rk, 1)
                    act.wait_ge(s_proj, 6 * c + 3 * ec + 2)
                    nc.scalar.activation(k_sb[:, ec, :], ps_r[:, 1, :], ACT.Copy,
                                         scale=x_scl[:, j, 3:4]).then_inc(s_rk, 1)

            def ysq(c):
                for ec in range(DC):
                    act.wait_ge(s_y, 2 * c + ec + 1)
                    nc.scalar.activation(y_sq[:, ec, :], y[:, ec, :], ACT.Square,
                                         accum_out=y_norm[:, 0, ec:ec + 1]).then_inc(s_ysq, 1)

            def yh(c):
                act.wait_ge(s_yscl, c + 1)
                nc.scalar.activation(y_hi[:, :, :], y[:, :, :], ACT.Copy, scale=y_scl[:, :]).then_inc(s_yh, 1)

            def x1h(c):
                act.wait_ge(s_t1, c + 1)
                nc.scalar.activation(x1_hi[:, :, :], ps_f[:, :, :], ACT.Copy, scale=X1S).then_inc(s_x1h, 1)

            def gelu(c, tiles=range(HC)):
                for hc in tiles:
                    act.wait_ge(s_f1, HC * c + hc + 1)
                    nc.scalar.activation(hid[:, hc, :], f1_bank[hc % NF], ACT.Gelu,
                                         bias=b1c[:, hc:hc + 1],
                                         scale=f1_scale[:, hc:hc + 1]).then_inc(s_gelu, 1)

            def hh(c, part):
                act.wait_ge(s_gelu, HC * c + part.stop)
                nc.scalar.activation(hid_hi[:, part, :], hid[:, part, :], ACT.Copy,
                                     scale=hid_scale[:, :]).then_inc(s_hh, part.stop - part.start)

            act.dma_start(lnw_c[:, :], ln_w.rearrange("(c p) -> p c", p=P),
                          allow_slow_non_contiguous=True).then_inc(s_small_in, 16)
            act.dma_start(dec_c[:, 0, :], decay.rearrange("(c p) -> p c", p=P),
                          allow_slow_non_contiguous=True).then_inc(s_small_in, 16)
            act.dma_start(b1c[:, :], b1.rearrange("(c p) -> p c", p=P),
                          allow_slow_non_contiguous=True).then_inc(s_small_in, 16)
            act.dma_start(b2r[:, :], b2.rearrange("(a d) -> a d", a=1).to_broadcast([P, D])).then_inc(s_small_in, 16)
            act.wait_ge(s_small_in, 64)
            nc.scalar.activation(dec_c[:, 1, :], dec_c[:, 0, :], ACT.Sigmoid).then_inc(s_setup_a, 1)
            xh(0, 0)
            act.wait_ge(s_setup_v, 1)
            nc.scalar.activation(dec_c[:, 2, :], dec_c[:, 1, :], ACT.Ln).then_inc(s_setup_a, 1)
            for n in range(3):
                act.wait_ge(s_setup_pe, n + 1)
                act.wait_ge(s_wscl, 1)
                nc.scalar.activation(proj_hi[:, n].rearrange("p c e -> p (c e)"), proj_bank[n], ACT.Copy,
                                     scale=w_scl[:, n:n + 1]).then_inc(s_proj_hi, 1)

            def clip_table(dc, part):
                nc.scalar.activation(clip_g[:, dc, part], steps[:, part], ACT.Exp, bias=log_clip[:, :],
                                     scale=dec_c[:, 2, dc:dc + 1]).then_inc(s_setup_a, 1)

            def wo_split_hi():
                act.wait_ge(s_setup_pe, 4)
                act.wait_ge(s_lnw, 1)
                for dc in range(DC):
                    nc.scalar.activation(wo_hi[:, dc, :], ps_s[:, dc * D:(dc + 1) * D], ACT.Copy,
                                         scale=lnw_scl[:, dc:dc + 1]).then_inc(s_wo_hi, 1)

            def alphas1():
                act.wait_ge(s_w1_in, 16)
                for hc in range(HC):
                    nc.scalar.activation(abs_w1[:, hc, :], w1_in[:, hc, :], ACT.Abs,
                                         accum_out=alpha1[:, hc:hc + 1]).then_inc(s_alpha, 1)

            def alphas2():
                act.wait_ge(s_w2_in, 16)
                for dc in range(DC):
                    nc.scalar.activation(abs_w2[:, dc, :], w2_in[:, dc, :], ACT.Abs,
                                         accum_out=alpha2[:, dc:dc + 1]).then_inc(s_alpha, 1)

            def w1_copies():
                act.wait_ge(s_setup_pe, 5)
                for dc in range(DC):
                    nc.scalar.activation(w1T[:, dc, :], ps_o[:, dc, :].bitcast(fp16), ACT.Copy).then_inc(s_wcopy, 1)

            def w2_copies():
                act.wait_ge(s_setup_pe, 6)
                for half in range(2):
                    dst = w2T[:, half * 4:half * 4 + 4, :].rearrange("p a d -> p (a d)")
                    nc.scalar.activation(dst, ps_f[:, half, :].bitcast(fp16), ACT.Copy).then_inc(s_wcopy, 1)

            def prologue():
                act.wait_ge(s_setup_a, 2)
                act.wait_ge(s_const, 1)
                for dc in range(DC):
                    clip_table(dc, slice(0, CH))
                rk(0, 0)
                xh(1, 1)
                wo_split_hi()
                ysq(0)
                w1_copies()
                yh(0)
                rk(1, 1, (0,))
                alphas1()
                alphas2()
                w2_copies()
                clip_table(0, slice(CH, T))
                rk(1, 1, (1,))
                clip_table(1, slice(CH, T))
                x1h(0)
                nc.scalar.activation(warm[:, :], ones_col[:, :], ACT.Gelu)
                xh(2, 2)
                ysq(1)
                act.wait_ge(s_ready, 1)
                gelu(0, range(4))
                yh(1)
                gelu(0, range(4, HC))
                act.wait_ge(s_ready, 2)
                for part in tile_groups(NCH):
                    hh(0, part)

            def step(i, b, j, left):
                if left > 2:
                    rk(i + 2, (j + 2) % CPB)
                    ysq(i + 2)
                if left > 1:
                    x1h(i + 1)
                if left > 2:
                    yh(i + 2)
                if left > 3:
                    xh(i + 3, (j + 3) % CPB)
                if left > 3:
                    gelu(i + 1)
                    for part in tile_groups(left - 1):
                        hh(i + 1, part)
                elif left > 1:
                    for part in tile_groups(left - 1):
                        gelu(i + 1, range(part.start, part.stop))
                        if part.start % 2 == 0:
                            hh(i + 1, part)

            steps_of(act, prologue, step)

        @block.vector
        def _(dve):
            def xmax(c, b, j):
                dve.wait_ge(s_x_in[j], 16 * b + 16)
                nc.vector.tensor_reduce(x_max[:, j, 0:1], x_in[j][:, :, :], AX.XY, ALU.max,
                                        apply_absolute_value=True).then_inc(s_xmax, 1)

            def xl(c, j):
                dve.wait_ge(s_xh, c + 1)
                nc.vector.scalar_tensor_tensor(out=x_lo[:, :, :], in0=ps_r[:, 0:DC, :], scalar=x_scl[:, j, 0:1],
                                               in1=x_hi[:, :, :], op0=ALU.mult,
                                               op1=ALU.subtract).then_inc(s_xl, 1)

            def kvs(c, j, ec):
                dve.wait_ge(s_proj, 6 * c + 3 * ec + 3)
                dve.wait_ge(s_rk, 4 * c + 2 * ec + 2)
                nc.vector.scalar_tensor_tensor(out=kv[:, ec, :], in0=ps_r[:, 2, :], scalar=x_scl[:, j, 4:5],
                                               in1=k_sb[:, ec, :], op0=ALU.mult,
                                               op1=ALU.mult).then_inc(s_kv, 1)

            def scans(c, j, ec):
                dve.wait_ge(s_kvg, 2 * c + ec + 1)
                first = state[(j + 1) % 2][:, ec, CH - 1:CH] if j % CPB else 0.0
                nc.vector.tensor_tensor_scan(state[j % 2][:, ec, :], decay_f[:, ec, :], kvg[:, ec, :], first,
                                             ALU.mult, ALU.add).then_inc(s_scan, 1)
                dve.wait_ge(s_scan, 2 * c + ec + 1)
                nc.vector.scalar_tensor_tensor(out=y[:, ec, :], in0=r_tanh[:, ec, :], scalar=1.0,
                                               in1=state[j % 2][:, ec, :], op0=ALU.add,
                                               op1=ALU.mult).then_inc(s_y, 1)

            def yl(c):
                dve.wait_ge(s_yh, c + 1)
                nc.vector.scalar_tensor_tensor(out=y_lo[:, :, :], in0=y[:, :, :], scalar=y_scl[:, :],
                                               in1=y_hi[:, :, :], op0=ALU.mult,
                                               op1=ALU.subtract).then_inc(s_yl, 1)

            def mean_sq(c):
                dve.wait_ge(s_sums, c + 1)
                nc.vector.tensor_scalar(ms[:, :], ps_s[:, 0:TT], 1.0 / D, 4.0 * EPS_RMS, ALU.mult,
                                        ALU.add).then_inc(s_ms, 1)

            def residual1(c, j, src=o_tok):
                dve.wait_ge(s_rms, c + 1)
                dve.wait_ge(s_o, c + 1)
                for tt in range(TT):
                    nc.vector.scalar_tensor_tensor(out=u[:, tt, :], in0=src[:, tt, :], scalar=rms[:, tt:tt + 1],
                                                   in1=x_in[j][:, tt, :], op0=ALU.mult,
                                                   op1=ALU.add).then_inc(s_u, 1)
                for tt in range(TT):
                    dve.wait_ge(s_u, TT * c + tt + 1)
                    nc.vector.bn_stats(u_st[:, tt, :], u[:, tt, :]).then_inc(s_ust, 1)
                dve.wait_ge(s_ust, TT * c + TT)
                stand_alone(dve)
                for tt in range(TT):
                    nc.vector.bn_aggr(u_mv[:, tt, :], u_st[:, tt, :]).then_inc(s_umv, 1)

            def norm1(c):
                dve.wait_ge(s_urstd, c + 1)
                for tt in range(TT):
                    nc.vector.tensor_scalar(x1[:, tt, :], u[:, tt, :], u_mv[:, tt, 0:1], u_rstd[:, tt:tt + 1],
                                            ALU.subtract, ALU.mult).then_inc(s_x1, 1)

            def x1l(c):
                dve.wait_ge(s_x1h, c + 1)
                nc.vector.scalar_tensor_tensor(out=x1_lo[:, :, :], in0=ps_f[:, :, :], scalar=X1S,
                                               in1=x1_hi[:, :, :], op0=ALU.mult,
                                               op1=ALU.subtract).then_inc(s_x1l, 1)

            def hl(c, part, tail=None):
                if tail is None:
                    dve.wait_ge(s_hh, HC * c + part.stop)
                elif part.start % 2 == 0:
                    dve.wait_ge(s_hh, HC * (NCH - 2) + HC // 2 * tail + part.start // 2 + 1)
                else:
                    dve.wait_ge(s_hh_odd, HC // 2 * tail + part.start // 2 + 1)
                nc.vector.scalar_tensor_tensor(out=hid_lo[:, part, :], in0=hid[:, part, :], scalar=hid_scale[:, :],
                                               in1=hid_hi[:, part, :], op0=ALU.mult,
                                               op1=ALU.subtract).then_inc(s_hl, part.stop - part.start)

            def zmul_last(c, j):
                for tt in range(TT):
                    dve.wait_ge(s_f2, 2 * c + tt // 2 + 1)
                    last = nc.vector.tensor_tensor(z[j % 2][:, tt, :], f2_last[tt], alpha2r[:, :], ALU.mult)
                    if tt % 2:
                        last.then_inc(s_zmul, 1)
                dve.wait_ge(s_zmul, 2 * c + 2)
                dve.wait_ge(s_x1b, c + 1)
                nc.vector.tensor_tensor(z[j % 2][:, 2:4, :], z[j % 2][:, 2:4, :], x1b[j % 2][:, 2:4, :],
                                        ALU.add).then_inc(s_zadd_last, 1)

            def zmul(c, j, halves=range(2)):
                for half in halves:
                    dve.wait_ge(s_f2, 2 * c + half + 1)
                    nc.vector.tensor_tensor(z[j % 2][:, 2 * half:2 * half + 2, :], o_tok[:, 2 * half:2 * half + 2, :],
                                            alpha2r[:, :].unsqueeze(1).to_broadcast([P, 2, D]),
                                            ALU.mult).then_inc(s_zmul, 1)

            def zstats(c, j, last_chunk=False):
                for tt in range(TT):
                    if last_chunk and tt >= TT // 2:
                        dve.wait_ge(s_zadd_last, 1)
                    else:
                        dve.wait_ge(s_zadd, 2 * c + tt // 2 + 1)
                    nc.vector.bn_stats(z_st[:, tt, :], z[j % 2][:, tt, :]).then_inc(s_zst, 1)
                dve.wait_ge(s_zst, TT * c + TT)
                stand_alone(dve)
                for tt in range(TT):
                    nc.vector.bn_aggr(z_mv[:, tt, :], z_st[:, tt, :]).then_inc(s_zmv, 1)

            def norm2(c, b, j):
                dve.wait_ge(s_zrstd, c + 1)
                dve.wait_ge(s_stored[j % 2], 16 * (2 * b + j // 2) + 16)
                for tt in range(TT):
                    nc.vector.tensor_scalar(z_out[j % 2][:, tt, :], z[j % 2][:, tt, :], z_mv[:, tt, 0:1],
                                            z_rstd[:, tt:tt + 1], ALU.subtract, ALU.mult).then_inc(s_zout, 1)

            chain = sem("dve_setup_chain")
            done = [0]

            def link(ins):
                done[0] += 1
                ins.then_inc(chain, 1)
                dve.wait_ge(chain, done[0])

            xmax(0, 0, 0)
            for n in range(3):
                dve.wait_ge(s_proj_in[n], 16)
                nc.vector.tensor_reduce(w_max[:, n:n + 1], proj_in[:, n], AX.XY, ALU.max,
                                        apply_absolute_value=True).then_inc(s_wmax, 1)
            dve.wait_ge(s_setup_a, 1)
            dve.wait_ge(s_small_in, 64)
            nc.vector.tensor_scalar_max(dec_c[:, 1, :], dec_c[:, 1, :], CLIP_DEC).then_inc(s_setup_v, 1)
            dve.wait_ge(s_wamax, 1)
            link(nc.vector.tensor_scalar_max(w_max[:, 0:3], w_amax[:, 0:3], TINY))
            link(nc.vector.reciprocal(w_scl[:, 0:3], w_max[:, 0:3]))
            nc.vector.tensor_scalar_mul(w_scl[:, 0:3], w_scl[:, 0:3], TOP).then_inc(s_wscl, 1)
            nc.vector.tensor_scalar_mul(w_inv[:, 0:1], w_max[:, 0:1], 0.5 / TOP)
            nc.vector.tensor_scalar_mul(w_inv[:, 1:3], w_max[:, 1:3], 1.0 / TOP).then_inc(s_winv, 1)
            xl(0, 0)
            for n in range(3):
                dve.wait_ge(s_proj_hi, n + 1)
                nc.vector.scalar_tensor_tensor(out=proj_lo[:, n].rearrange("p c e -> p (c e)"), in0=proj_bank[n],
                                               scalar=w_scl[:, n:n + 1],
                                               in1=proj_hi[:, n].rearrange("p c e -> p (c e)"), op0=ALU.mult,
                                               op1=ALU.subtract).then_inc(s_setup_ev, 1)

            def decay_rows():
                dve.wait_ge(s_const, 1)
                for dc in range(DC):
                    nc.vector.tensor_scalar(decay_f[:, dc, :], steps[:, 0:CH], 0.0, dec_c[:, 1, dc:dc + 1],
                                            ALU.mult, ALU.add)

            def wo_maxima():
                dve.wait_ge(s_wo_in, 16)
                nc.vector.tensor_reduce(w_max[:, 3:4], wo_in[:, :, :], AX.XY, ALU.max,
                                        apply_absolute_value=True).then_inc(s_wmax, 1)
                nc.vector.tensor_reduce(w_max[:, 4:5], lnw_c[:, :], AX.X, ALU.max,
                                        apply_absolute_value=True).then_inc(s_wmax, 1)

            def wo_scale():
                dve.wait_ge(s_wamax, 2)
                link(nc.vector.tensor_scalar_max(w_max[:, 3:5], w_amax[:, 3:5], TINY_ROOT))
                link(nc.vector.tensor_scalar(w_max[:, 3:4], w_max[:, 3:4], w_max[:, 4:5], 1.0 / TOP, ALU.mult,
                                             ALU.mult))
                nc.vector.tensor_copy(wo_inv[:, :], w_max[:, 3:4])
                link(nc.vector.reciprocal(w_scl[:, 3:4], w_max[:, 3:4]))
                nc.vector.tensor_scalar(lnw_scl[:, :], lnw_c[:, :], w_scl[:, 3:4], None, ALU.mult).then_inc(s_lnw, 1)

            def wo_split_lo():
                dve.wait_ge(s_wo_hi, DC)
                for dc in range(DC):
                    last = nc.vector.scalar_tensor_tensor(out=wo_lo[:, dc, :], in0=ps_s[:, dc * D:(dc + 1) * D],
                                                          scalar=lnw_scl[:, dc:dc + 1], in1=wo_hi[:, dc, :],
                                                          op0=ALU.mult, op1=ALU.subtract)
                last.then_inc(s_setup_v, 1)

            def sign(src, dst, landed):
                dve.wait_ge(landed, 16)
                link(nc.vector.tensor_scalar(dst[:, :, :], src[:, :, :], 0.0, None, ALU.is_lt))
                nc.vector.scalar_tensor_tensor(out=dst[:, :, :], in0=src[:, :, :], scalar=0.0, in1=dst[:, :, :],
                                               op0=ALU.is_gt, op1=ALU.subtract).then_inc(s_sgn, 1)

            def hidden_bound():
                dve.wait_ge(s_alpha, HC + DC)
                link(nc.vector.scalar_tensor_tensor(out=hid_bound[:, 0, :], in0=b1c[:, :], scalar=-1.0,
                                                    in1=b1c[:, :], op0=ALU.mult, op1=ALU.max))
                link(nc.vector.tensor_tensor(hid_bound[:, 1, :], hid_bound[:, 0, :], alpha1[:, :], ALU.add))
                nc.vector.tensor_reduce(w_max[:, 5:6], hid_bound[:, 1, :], AX.X, ALU.max).then_inc(s_wmax, 1)
                nc.vector.tensor_scalar_mul(f1_scale[:, :], alpha1[:, :], 1.0 / (D * X1S)).then_inc(s_ready, 1)

            def hidden_scale():
                dve.wait_ge(s_wamax, 3)
                link(nc.vector.tensor_scalar_max(w_max[:, 5:6], w_amax[:, 5:6], TINY))
                link(nc.vector.reciprocal(w_scl[:, 5:6], w_max[:, 5:6]))
                nc.vector.tensor_scalar_mul(hid_scale[:, :], w_scl[:, 5:6], HTOP).then_inc(s_ready, 1)
                link(nc.vector.tensor_scalar(alpha2[:, :], alpha2[:, :], w_max[:, 5:6], 1.0 / (H * HTOP), ALU.mult,
                                             ALU.mult))
                for dc in range(DC):
                    last = nc.vector.tensor_scalar(alpha2_sq[:, dc, :], ones_sq[:, :], alpha2[:, dc:dc + 1], None,
                                                   ALU.mult)
                last.then_inc(s_setup_v, 1)

            def alpha_rows():
                dve.wait_ge(s_setup_pe, 7)
                nc.vector.tensor_copy(alpha2r[:, :], ps_s[:, 0:D]).then_inc(s_alpha, 1)
                dve.wait_ge(s_alpha, HC + DC + 1)

            def clip_min(n, part, dcs=range(DC)):
                for dc in dcs:
                    dve.wait_ge(s_setup_a, 3 + DC * n + dc)
                    nc.vector.tensor_scalar_min(clip_g[:, dc, part], clip_g[:, dc, part], 1.0).then_inc(s_clip, 1)

            def prologue():
                decay_rows()
                clip_min(0, slice(0, CH))
                xmax(1, 0, 1)
                wo_maxima()
                kvs(0, 0, 0)
                sign(w1_in, w1_sgn, s_w1_in)
                kvs(0, 0, 1)
                wo_scale()
                scans(0, 0, 0)
                scans(0, 0, 1)
                xl(1, 1)
                wo_split_lo()
                sign(w2_in, w2_sgn, s_w2_in)
                yl(0)
                kvs(1, 1, 0)
                mean_sq(0)
                xmax(2, 0, 2)
                residual1(0, 0)
                hidden_bound()
                clip_min(1, slice(CH, T), (0,))
                kvs(1, 1, 1)
                norm1(0)
                scans(1, 1, 0)
                clip_min(1, slice(CH, T), (1,))
                x1l(0)
                hidden_scale()
                scans(1, 1, 1)
                alpha_rows()
                xl(2, 2)
                xmax(3, 0, 3)
                yl(1)
                mean_sq(1)
                hl(0, tile_groups(NCH)[0])

            def step(i, b, j, left):
                if left > 1:
                    residual1(i + 1, (j + 1) % CPB, o_tok if left > 2 else o_last)
                if left == 2:
                    for part in tile_groups(left)[4:]:
                        hl(i, part, 0)
                parts = tile_groups(left)
                if left > 2:
                    kvs(i + 2, (j + 2) % CPB, 0)
                    hl(i, parts[1])
                    scans(i + 2, (j + 2) % CPB, 0)
                    kvs(i + 2, (j + 2) % CPB, 1)
                if left > 1:
                    norm1(i + 1)
                if left == 2:
                    norm2(i - 1, b, j - 1)
                if left > 2:
                    scans(i + 2, (j + 2) % CPB, 1)
                if left > 1:
                    zmul(i, j, (0,))
                if left > 4:
                    xmax(i + 4, b + 1, j)
                if left > 1:
                    x1l(i + 1)
                if left > 2:
                    yl(i + 2)
                if left > 1:
                    zmul(i, j, (1,))
                else:
                    zmul_last(i, j)
                if left > 3:
                    xl(i + 3, (j + 3) % CPB)
                zstats(i, j, left == 1)
                if left == 3:
                    mean_sq(i + 2)
                    for part in tile_groups(left - 1)[:4]:
                        hl(i + 1, part, 0)
                if left == 2:
                    for part in tile_groups(left - 1):
                        hl(i + 1, part, 1)
                if left != 3:
                    norm2(i, b, j)
                if left > 3:
                    mean_sq(i + 2)
                    hl(i + 1, tile_groups(left - 1)[0])

            steps_of(dve, prologue, step)

        @block.gpsimd
        def _(pool):
            def scales(c, j):
                pool.wait_ge(s_xmax, c + 1)
                stand_alone(pool)
                nc.gpsimd.partition_all_reduce(x_max[:, j, 1:2], x_max[:, j, 0:1], P, RMAX).then_inc(s_xamax, 1)
                pool.wait_ge(s_xamax, c + 1)
                stand_alone(pool)
                nc.gpsimd.tensor_scalar(x_scl[:, j, 1:2], x_max[:, j, 1:2], TINY, 1.0 / TOP, ALU.max,
                                        ALU.mult).then_inc(s_xtmp, 1)
                pool.wait_ge(s_xtmp, c + 1)
                nc.gpsimd.tensor_tensor(x_scl[:, j, 0:1], x_scl[:, j, 1:2], neg_one[:, :], ALU.pow).then_inc(s_xscl, 1)

            def unscales(c, j):
                nc.gpsimd.tensor_tensor(x_scl[:, j, 2:5], w_inv[:, :],
                                        x_scl[:, j, 1:2].to_broadcast([P, 3]), ALU.mult).then_inc(s_xun, 1)

            def gate(c, j, ecs=range(DC)):
                for ec in ecs:
                    pool.wait_ge(s_kv, 2 * c + ec + 1)
                    nc.gpsimd.tensor_tensor(kvg[:, ec, :], kv[:, ec, :], clip_g[:, ec, j * CH:(j + 1) * CH],
                                            ALU.mult).then_inc(s_kvg, 1)

            def y_scale(c):
                pool.wait_ge(s_ysq, 2 * c + 2)
                stand_alone(pool)
                nc.gpsimd.partition_all_reduce(y_norm[:, 1, :], y_norm[:, 0, :], P, RMAX).then_inc(s_ynorm, 1)
                pool.wait_ge(s_ynorm, c + 1)
                nc.gpsimd.tensor_tensor(y_q[:, 0:1], y_norm[:, 1, 0:1], y_norm[:, 1, 1:2], ALU.add).then_inc(s_yq, 1)
                pool.wait_ge(s_yq, c + 1)
                stand_alone(pool)
                nc.gpsimd.tensor_scalar(y_q[:, 1:2], y_q[:, 0:1], 1.0 / YTOP ** 2, TINY, ALU.mult,
                                        ALU.max).then_inc(s_yq2, 1)
                pool.wait_ge(s_yq2, c + 1)
                nc.gpsimd.tensor_tensor(y_scl[:, :], y_q[:, 1:2], neg_half[:, 0:1], ALU.pow).then_inc(s_yscl, 1)
                nc.gpsimd.tensor_tensor(y_inv[:, 0:1], y_q[:, 1:2], half_one[:, :], ALU.pow).then_inc(s_yinv, 1)
                pool.wait_ge(s_yinv, c + 1)
                nc.gpsimd.tensor_tensor(y_inv[:, 1:2], y_inv[:, 0:1], wo_inv[:, :], ALU.mult).then_inc(s_yinv2, 1)

            def ysqs(c):
                pool.wait_ge(s_ysq, 2 * c + 2)
                nc.gpsimd.tensor_tensor(y_sqs[:, :], y_sq[:, 0, :], y_sq[:, 1, :], ALU.add).then_inc(s_ysqs, 1)

            def root_rms(c):
                pool.wait_ge(s_ms, c + 1)
                nc.gpsimd.tensor_tensor(root[:, :], ms[:, :], neg_half[:, :], ALU.pow).then_inc(s_root, 1)
                pool.wait_ge(s_root, c + 1)
                pool.wait_ge(s_yinv2, c + 1)
                nc.gpsimd.tensor_tensor(rms[:, :], root[:, :], y_inv[:, 1:2].to_broadcast([P, TT]),
                                        ALU.mult).then_inc(s_rms, 1)

            def root_u(c):
                pool.wait_ge(s_umv, TT * c + TT)
                stand_alone(pool)
                nc.gpsimd.tensor_scalar(u_ve[:, :], u_mv[:, :, 1], EPS_LN, 1.0, ALU.add, ALU.mult).then_inc(s_uve, 1)
                pool.wait_ge(s_uve, c + 1)
                nc.gpsimd.tensor_tensor(u_rstd[:, :], u_ve[:, :], neg_half[:, :], ALU.pow).then_inc(s_urstd, 1)

            def add_b2(c, j):
                pool.wait_ge(s_x1, TT * c + TT)
                nc.gpsimd.tensor_tensor(x1b[j % 2][:, :, :], x1[:, :, :],
                                        b2r[:, :].unsqueeze(1).to_broadcast([P, TT, D]),
                                        ALU.add).then_inc(s_x1b, 1)

            def hh_odd(c, part):
                pool.wait_ge(s_gelu, HC * c + part.stop)
                nc.gpsimd.tensor_scalar(hid_hi[:, part, :], hid[:, part, :], hid_scale[:, :], 1.0, ALU.mult,
                                        ALU.mult).then_inc(s_hh_odd, 1)

            def zadd(c, j, halves):
                pool.wait_ge(s_x1b, c + 1)
                for half in range(halves):
                    pool.wait_ge(s_zmul, 2 * c + half + 1)
                    part = z[j % 2][:, 2 * half:2 * half + 2, :]
                    nc.gpsimd.tensor_tensor(part, part, x1b[j % 2][:, 2 * half:2 * half + 2, :],
                                            ALU.add).then_inc(s_zadd, 1)

            def root_z(c):
                pool.wait_ge(s_zmv, TT * c + TT)
                stand_alone(pool)
                nc.gpsimd.tensor_scalar(z_ve[:, :], z_mv[:, :, 1], EPS_LN, 1.0, ALU.add, ALU.mult).then_inc(s_zve, 1)
                pool.wait_ge(s_zve, c + 1)
                nc.gpsimd.tensor_tensor(z_rstd[:, :], z_ve[:, :], neg_half[:, :], ALU.pow).then_inc(s_zrstd, 1)

            nc.gpsimd.memset(ident[:, :], 0.0).then_inc(s_zeroed, 1)
            nc.gpsimd.memset(ident16[:, :], 0.0).then_inc(s_zeroed, 1)
            nc.gpsimd.memset(ones_col[:, :], 1.0)
            nc.gpsimd.memset(ones_sq[:, :], 1.0)
            nc.gpsimd.memset(neg_half[:, :], -0.5)
            nc.gpsimd.memset(neg_one[:, :], -1.0)
            nc.gpsimd.memset(half_one[:, :], 0.5)
            pool.wait_ge(s_zeroed, 2)
            for m in (ident, ident16):
                nc.gpsimd.affine_select(out=m[:, :], in_=m[:, :], compare_op=ALU.not_equal, fill=1.0, base=0,
                                        pattern=[[-1, P]], channel_multiplier=1).then_inc(s_ident, 1)
            nc.gpsimd.memset(log_clip[:, :], LOG_CLIP)
            nc.gpsimd.iota(steps[:, :], [[1, T]], base=0, channel_multiplier=0,
                           allow_small_or_imprecise_dtypes=True).then_inc(s_const, 1)
            scales(0, 0)
            pool.wait_ge(s_wmax, 3)
            nc.gpsimd.partition_all_reduce(w_amax[:, 0:3], w_max[:, 0:3], P, RMAX).then_inc(s_wamax, 1)

            def prologue():
                pool.wait_ge(s_winv, 1)
                unscales(0, 0)
                scales(1, 1)
                unscales(1, 1)
                pool.wait_ge(s_wmax, 5)
                nc.gpsimd.partition_all_reduce(w_amax[:, 3:5], w_max[:, 3:5], P, RMAX).then_inc(s_wamax, 1)
                pool.wait_ge(s_clip, DC)
                gate(0, 0)
                pool.wait_ge(s_lnw, 1)
                y_scale(0)
                ysqs(0)
                root_rms(0)
                scales(2, 2)
                unscales(2, 2)
                root_u(0)
                pool.wait_ge(s_wmax, 6)
                nc.gpsimd.partition_all_reduce(w_amax[:, 5:6], w_max[:, 5:6], P, RMAX).then_inc(s_wamax, 1)
                pool.wait_ge(s_clip, DC + 1)
                gate(1, 1, (0,))
                pool.wait_ge(s_clip, 2 * DC)
                gate(1, 1, (1,))
                y_scale(1)
                ysqs(1)
                add_b2(0, 0)
                scales(3, 3)
                unscales(3, 3)
                root_rms(1)

            def step(i, b, j, left):
                if left > 1:
                    root_u(i + 1)
                if left > 2:
                    gate(i + 2, (j + 2) % CPB)
                if left > 1:
                    add_b2(i + 1, j + 1)
                if left > 2:
                    y_scale(i + 2)
                    ysqs(i + 2)
                zadd(i, j, 2 if left > 1 else 1)
                if left > 4:
                    scales(i + 4, j)
                    unscales(i + 4, j)
                odd = tile_groups(left - 1)[1::2] if left in (2, 3) else ()
                if left == 3:
                    root_rms(i + 2)
                    for part in odd[:2]:
                        hh_odd(i + 1, part)
                root_z(i)
                for part in odd[2:] if left == 3 else odd:
                    hh_odd(i + 1, part)
                if left > 3:
                    root_rms(i + 2)

            steps_of(pool, prologue, step)


_INS = ['L0_attn_x', 'L0_attn_Wr', 'L0_attn_Wk', 'L0_attn_Wv', 'L0_attn_Wo', 'L0_attn_decay', 'L0_attn_ln_w',
        'L0_ffn_w1', 'L0_ffn_b1', 'L0_ffn_w2', 'L0_ffn_b2']
_OUTS = [((8, 2048, 256), 'float32')]


def kernel(**inputs):
    import numpy as _np
    import concourse.bacc as _bacc
    from concourse import mybir as _mybir
    from concourse.bass_utils import run_bass_kernel_spmd as _run

    nc = _bacc.Bacc("TRN2", target_bir_lowering=False, num_devices=1)
    arrays, args = {}, []
    for name in _INS:
        a = _np.ascontiguousarray(inputs[name])
        arrays[f"in_{name}_dram"] = a
        args.append(nc.dram_tensor(f"in_{name}_dram", a.shape, _mybir.dt.from_np(a.dtype), kind="ExternalInput").ap())
    for i, (shape, dtype) in enumerate(_OUTS):
        dt = _mybir.dt.from_np(_np.dtype(dtype))
        args.append(nc.dram_tensor(f"out_{i}_dram", shape, dt, kind="ExternalOutput").ap())
    postln_layer_kernel(nc, *args)
    r = _run(nc, [arrays], core_ids=[0])
    got = tuple(r.results[0][f"out_{i}_dram"] for i in range(len(_OUTS)))
    return got[0]
```
